# Optimizing a Trainium2 kernel written in Bass

```python
import numpy as np
import jax
import jax.numpy as jnp

def _softmax(x, axis=-1):
    return jax.nn.softmax(x, axis=axis)

def _gelu(x):
    return jax.nn.gelu(x, approximate=True)

def _silu(x):
    return jax.nn.silu(x)

def _sigmoid(x):
    return jax.nn.sigmoid(x)

def _layernorm(x, axis=-1, eps=1e-05):
    m = jnp.mean(x, axis=axis, keepdims=True)
    v = jnp.var(x, axis=axis, keepdims=True)
    return (x - m) / jnp.sqrt(v + eps)

def _scatter_add(tgt, idx, src, axis=0):
    return tgt.at[idx].add(src)

def _segment_sum(src, seg, n):
    return jax.ops.segment_sum(src, seg, n)
kernel_name = 'mk_xattn_seq_d2_seqx_r4_71e0de'

def setup_inputs(seed: int=0):
    np.random.seed(seed)
    _w = jnp.asarray

    def _rec_inputs():
        import jax
        import jax.numpy as jnp
        _rk = jax.random.key(seed)
        x = -0.0002928 + 1 * jax.random.normal(jax.random.fold_in(_rk, 1), (1, 2048, 256), jnp.float32)
        _lenS = 2048 - jax.random.randint(jax.random.fold_in(_rk, 7), (1,), 0, max(1, 2048 // 4) + 1, jnp.int32)
        _lenS2 = 1601 - jax.random.randint(jax.random.fold_in(_rk, 8), (1,), 0, max(1, 1601 // 4) + 1, jnp.int32)
        _ctx_1024P = jax.random.normal(jax.random.fold_in(_rk, 11), (1, 16, 256), jnp.float32)
        _ctx_1024c = jax.random.dirichlet(jax.random.fold_in(_rk, 511), 0.3 * jnp.ones((16,), jnp.float32), (1, 1601))
        _ctx_1024t = jnp.einsum('bsk,bkd->bsd', _ctx_1024c, _ctx_1024P)
        _ctx_1024t = _ctx_1024t * jax.lax.rsqrt(jnp.mean(jnp.square(_ctx_1024t)) + 1e-12) * 0.953939
        ctx_1024 = 0.0061147 + 1.02565 * (_ctx_1024t + 0.3 * jax.random.normal(jax.random.fold_in(_rk, 611), (1, 1601, 256), jnp.float32))
        _validS = jnp.arange(2048)[None, :] < _lenS[:, None]
        _validS2 = jnp.arange(1601)[None, :] < _lenS2[:, None]
        _causal = jnp.tril(jnp.ones((2048, 2048), dtype=bool))
        mask_1x1xSxS_ik0 = jnp.where(jnp.broadcast_to(_validS[0:1, None, None, :], (1, 1, 2048, 2048)), 0, 1).astype(jnp.int32)
        return (x, ctx_1024, mask_1x1xSxS_ik0)
    x, ctx_1024, mask_1x1xSxS_ik0 = _rec_inputs()

    def _L0_xattn_setup():
        import jax, jax.numpy as jnp
        import numpy as np
        EPS = 1e-06
        H = 16

        def _ln(x):
            mu = jnp.mean(x, axis=-1, keepdims=True)
            var = jnp.mean(jnp.square(x - mu), axis=-1, keepdims=True)
            return (x - mu) / jnp.sqrt(var + EPS)

        def _mod(x, shift, scale):
            return x * (1.0 + scale[:, None, :]) + shift[:, None, :]

        def _heads(x, qkv_w, qkv_b):
            B, N, C = x.shape
            hd = C // H
            qkv = (x @ qkv_w + qkv_b).reshape(B, N, 3, H, hd).transpose(2, 0, 3, 1, 4)
            return (qkv[0], qkv[1], qkv[2])

        def _attend(q, k, v):
            sc = q.shape[-1] ** (-0.5)
            a = jax.nn.softmax(jnp.einsum('bhnd,bhmd->bhnm', q, k) * sc, axis=-1)
            o = jnp.einsum('bhnm,bhmd->bhnd', a, v)
            B, h, N, hd = o.shape
            return o.transpose(0, 2, 1, 3).reshape(B, N, h * hd)

        def _mha(x, qkv_w, qkv_b, proj_w, proj_b):
            q, k, v = _heads(x, qkv_w, qkv_b)
            return _attend(q, k, v) @ proj_w + proj_b
        key = jax.random.key(seed)
        ks = jax.random.split(key, 16)
        B, T, D = (2, 512, 256)
        Dh = 4 * D
        s = 0.02
        return {'x': jax.random.normal(ks[0], (B, T, D), jnp.float32), 'c': jax.random.normal(ks[1], (B, 2, D), jnp.float32), 'attn_qkv_w': jax.random.normal(ks[2], (D, 3 * D), jnp.float32) * s, 'attn_qkv_b': jnp.zeros((3 * D,), jnp.float32), 'attn_proj_w': jax.random.normal(ks[3], (D, D), jnp.float32) * s, 'attn_proj_b': jnp.zeros((D,), jnp.float32), 'crs_qkv_w': jax.random.normal(ks[4], (D, 3 * D), jnp.float32) * s, 'crs_qkv_b': jnp.zeros((3 * D,), jnp.float32), 'crs_proj_w': jax.random.normal(ks[5], (D, D), jnp.float32) * s, 'crs_proj_b': jnp.zeros((D,), jnp.float32), 'mlp_fc1_w': jax.random.normal(ks[6], (D, Dh), jnp.float32) * s, 'mlp_fc1_b': jnp.zeros((Dh,), jnp.float32), 'mlp_fc2_w': jax.random.normal(ks[7], (Dh, D), jnp.float32) * s, 'mlp_fc2_b': jnp.zeros((D,), jnp.float32), 'ada_w': jax.random.normal(ks[8], (D, 9 * D), jnp.float32) * s, 'ada_b': jnp.zeros((9 * D,), jnp.float32)}
    _L0_xattn_all = _L0_xattn_setup()
    _L0_xattn_in = {k: v for k, v in _L0_xattn_all.items() if k in ('attn_qkv_w', 'attn_qkv_b', 'attn_proj_w', 'attn_proj_b', 'crs_qkv_w', 'crs_qkv_b', 'crs_proj_w', 'crs_proj_b', 'mlp_fc1_w', 'mlp_fc1_b', 'mlp_fc2_w', 'mlp_fc2_b', 'ada_w', 'ada_b')}
    del _L0_xattn_all

    def _L1_xattn_setup():
        import jax, jax.numpy as jnp
        import numpy as np
        D_MODEL = 256
        NHEAD = 16
        D_FF = 1024
        B = 2
        S = 512
        EPS = 1e-05

        def _mha(q_in, k_in, v_in, qw, qb, kw, kb, vw, vb, ow, ob, mask):
            b, sq, d = q_in.shape
            sk = k_in.shape[1]
            hd = d // NHEAD
            q = (q_in @ qw + qb).reshape(b, sq, NHEAD, hd).transpose(0, 2, 1, 3)
            k = (k_in @ kw + kb).reshape(b, sk, NHEAD, hd).transpose(0, 2, 1, 3)
            v = (v_in @ vw + vb).reshape(b, sk, NHEAD, hd).transpose(0, 2, 1, 3)
            scores = jnp.einsum('bhqd,bhkd->bhqk', q, k) / jnp.sqrt(jnp.float32(hd))
            if mask is not None:
                scores = jnp.where(mask == 0, jnp.float32(-1000000000.0), scores)
            attn = jax.nn.softmax(scores, axis=-1)
            out = jnp.einsum('bhqk,bhkd->bhqd', attn, v)
            out = out.transpose(0, 2, 1, 3).reshape(b, sq, d)
            return out @ ow + ob

        def _layernorm(x, g, b):
            mu = jnp.mean(x, axis=-1, keepdims=True)
            var = jnp.var(x, axis=-1, keepdims=True)
            return (x - mu) * jax.lax.rsqrt(var + EPS) * g + b
        key = jax.random.key(seed)
        ks = jax.random.split(key, 16)
        sc = 0.02
        inp = {'tgt': jax.random.normal(ks[0], (B, S, D_MODEL), jnp.float32), 'memory': jax.random.normal(ks[1], (B, S, D_MODEL), jnp.float32), 'tgt_mask': jnp.tril(jnp.ones((S, S), jnp.int32))[None, None, :, :], 'sa_qw': jax.random.normal(ks[2], (D_MODEL, D_MODEL), jnp.float32) * sc, 'sa_qb': jnp.zeros((D_MODEL,), jnp.float32), 'sa_kw': jax.random.normal(ks[3], (D_MODEL, D_MODEL), jnp.float32) * sc, 'sa_kb': jnp.zeros((D_MODEL,), jnp.float32), 'sa_vw': jax.random.normal(ks[4], (D_MODEL, D_MODEL), jnp.float32) * sc, 'sa_vb': jnp.zeros((D_MODEL,), jnp.float32), 'sa_ow': jax.random.normal(ks[5], (D_MODEL, D_MODEL), jnp.float32) * sc, 'sa_ob': jnp.zeros((D_MODEL,), jnp.float32), 'ca_qw': jax.random.normal(ks[6], (D_MODEL, D_MODEL), jnp.float32) * sc, 'ca_qb': jnp.zeros((D_MODEL,), jnp.float32), 'ca_kw': jax.random.normal(ks[7], (D_MODEL, D_MODEL), jnp.float32) * sc, 'ca_kb': jnp.zeros((D_MODEL,), jnp.float32), 'ca_vw': jax.random.normal(ks[8], (D_MODEL, D_MODEL), jnp.float32) * sc, 'ca_vb': jnp.zeros((D_MODEL,), jnp.float32), 'ca_ow': jax.random.normal(ks[9], (D_MODEL, D_MODEL), jnp.float32) * sc, 'ca_ob': jnp.zeros((D_MODEL,), jnp.float32), 'w1': jax.random.normal(ks[10], (D_MODEL, D_FF), jnp.float32) * sc, 'b1': jnp.zeros((D_FF,), jnp.float32), 'w2': jax.random.normal(ks[11], (D_FF, D_MODEL), jnp.float32) * sc, 'b2': jnp.zeros((D_MODEL,), jnp.float32), 'g1': jnp.ones((D_MODEL,), jnp.float32), 'be1': jnp.zeros((D_MODEL,), jnp.float32), 'g2': jnp.ones((D_MODEL,), jnp.float32), 'be2': jnp.zeros((D_MODEL,), jnp.float32), 'g3': jnp.ones((D_MODEL,), jnp.float32), 'be3': jnp.zeros((D_MODEL,), jnp.float32)}
        return inp
    _L1_xattn_all = _L1_xattn_setup()
    _L1_xattn_in = {k: v for k, v in _L1_xattn_all.items() if k in ('sa_qw', 'sa_qb', 'sa_kw', 'sa_kb', 'sa_vw', 'sa_vb', 'sa_ow', 'sa_ob', 'ca_qw', 'ca_qb', 'ca_kw', 'ca_kb', 'ca_vw', 'ca_vb', 'ca_ow', 'ca_ob', 'w1', 'b1', 'w2', 'b2', 'g1', 'be1', 'g2', 'be2', 'g3', 'be3')}
    del _L1_xattn_all
    return {'x': x, 'ctx_1024': ctx_1024, 'mask_1x1xSxS_ik0': mask_1x1xSxS_ik0, 'L0_xattn_attn_qkv_w': _L0_xattn_in['attn_qkv_w'], 'L0_xattn_attn_qkv_b': _L0_xattn_in['attn_qkv_b'], 'L0_xattn_attn_proj_w': _L0_xattn_in['attn_proj_w'], 'L0_xattn_attn_proj_b': _L0_xattn_in['attn_proj_b'], 'L0_xattn_crs_qkv_w': _L0_xattn_in['crs_qkv_w'], 'L0_xattn_crs_qkv_b': _L0_xattn_in['crs_qkv_b'], 'L0_xattn_crs_proj_w': _L0_xattn_in['crs_proj_w'], 'L0_xattn_crs_proj_b': _L0_xattn_in['crs_proj_b'], 'L0_xattn_mlp_fc1_w': _L0_xattn_in['mlp_fc1_w'], 'L0_xattn_mlp_fc1_b': _L0_xattn_in['mlp_fc1_b'], 'L0_xattn_mlp_fc2_w': _L0_xattn_in['mlp_fc2_w'], 'L0_xattn_mlp_fc2_b': _L0_xattn_in['mlp_fc2_b'], 'L0_xattn_ada_w': _L0_xattn_in['ada_w'], 'L0_xattn_ada_b': _L0_xattn_in['ada_b'], 'L1_xattn_sa_qw': _L1_xattn_in['sa_qw'], 'L1_xattn_sa_qb': _L1_xattn_in['sa_qb'], 'L1_xattn_sa_kw': _L1_xattn_in['sa_kw'], 'L1_xattn_sa_kb': _L1_xattn_in['sa_kb'], 'L1_xattn_sa_vw': _L1_xattn_in['sa_vw'], 'L1_xattn_sa_vb': _L1_xattn_in['sa_vb'], 'L1_xattn_sa_ow': _L1_xattn_in['sa_ow'], 'L1_xattn_sa_ob': _L1_xattn_in['sa_ob'], 'L1_xattn_ca_qw': _L1_xattn_in['ca_qw'], 'L1_xattn_ca_qb': _L1_xattn_in['ca_qb'], 'L1_xattn_ca_kw': _L1_xattn_in['ca_kw'], 'L1_xattn_ca_kb': _L1_xattn_in['ca_kb'], 'L1_xattn_ca_vw': _L1_xattn_in['ca_vw'], 'L1_xattn_ca_vb': _L1_xattn_in['ca_vb'], 'L1_xattn_ca_ow': _L1_xattn_in['ca_ow'], 'L1_xattn_ca_ob': _L1_xattn_in['ca_ob'], 'L1_xattn_w1': _L1_xattn_in['w1'], 'L1_xattn_b1': _L1_xattn_in['b1'], 'L1_xattn_w2': _L1_xattn_in['w2'], 'L1_xattn_b2': _L1_xattn_in['b2'], 'L1_xattn_g1': _L1_xattn_in['g1'], 'L1_xattn_be1': _L1_xattn_in['be1'], 'L1_xattn_g2': _L1_xattn_in['g2'], 'L1_xattn_be2': _L1_xattn_in['be2'], 'L1_xattn_g3': _L1_xattn_in['g3'], 'L1_xattn_be3': _L1_xattn_in['be3']}

def reference(x, ctx_1024, mask_1x1xSxS_ik0, L0_xattn_attn_qkv_w, L0_xattn_attn_qkv_b, L0_xattn_attn_proj_w, L0_xattn_attn_proj_b, L0_xattn_crs_qkv_w, L0_xattn_crs_qkv_b, L0_xattn_crs_proj_w, L0_xattn_crs_proj_b, L0_xattn_mlp_fc1_w, L0_xattn_mlp_fc1_b, L0_xattn_mlp_fc2_w, L0_xattn_mlp_fc2_b, L0_xattn_ada_w, L0_xattn_ada_b, L1_xattn_sa_qw, L1_xattn_sa_qb, L1_xattn_sa_kw, L1_xattn_sa_kb, L1_xattn_sa_vw, L1_xattn_sa_vb, L1_xattn_sa_ow, L1_xattn_sa_ob, L1_xattn_ca_qw, L1_xattn_ca_qb, L1_xattn_ca_kw, L1_xattn_ca_kb, L1_xattn_ca_vw, L1_xattn_ca_vb, L1_xattn_ca_ow, L1_xattn_ca_ob, L1_xattn_w1, L1_xattn_b1, L1_xattn_w2, L1_xattn_b2, L1_xattn_g1, L1_xattn_be1, L1_xattn_g2, L1_xattn_be2, L1_xattn_g3, L1_xattn_be3):
    import jax
    import jax.numpy as jnp

    def _L0_xattn_ref(x, c, attn_qkv_w, attn_qkv_b, attn_proj_w, attn_proj_b, crs_qkv_w, crs_qkv_b, crs_proj_w, crs_proj_b, mlp_fc1_w, mlp_fc1_b, mlp_fc2_w, mlp_fc2_b, ada_w, ada_b):
        import jax, jax.numpy as jnp
        import numpy as np
        EPS = 1e-06
        H = 16

        def _ln(x):
            mu = jnp.mean(x, axis=-1, keepdims=True)
            var = jnp.mean(jnp.square(x - mu), axis=-1, keepdims=True)
            return (x - mu) / jnp.sqrt(var + EPS)

        def _mod(x, shift, scale):
            return x * (1.0 + scale[:, None, :]) + shift[:, None, :]

        def _heads(x, qkv_w, qkv_b):
            B, N, C = x.shape
            hd = C // H
            qkv = (x @ qkv_w + qkv_b).reshape(B, N, 3, H, hd).transpose(2, 0, 3, 1, 4)
            return (qkv[0], qkv[1], qkv[2])

        def _attend(q, k, v):
            sc = q.shape[-1] ** (-0.5)
            a = jax.nn.softmax(jnp.einsum('bhnd,bhmd->bhnm', q, k) * sc, axis=-1)
            o = jnp.einsum('bhnm,bhmd->bhnd', a, v)
            B, h, N, hd = o.shape
            return o.transpose(0, 2, 1, 3).reshape(B, N, h * hd)

        def _mha(x, qkv_w, qkv_b, proj_w, proj_b):
            q, k, v = _heads(x, qkv_w, qkv_b)
            return _attend(q, k, v) @ proj_w + proj_b
        mod = jax.nn.silu(c) @ ada_w + ada_b
        sh_msa, sc_msa, g_msa, sh_mca, sc_mca, g_mca, sh_mlp, sc_mlp, g_mlp = jnp.split(mod, 9, axis=2)
        B, T, D = x.shape
        h = T // 2
        x0, x1 = (x[:, :h], x[:, h:])
        x0 = x0 + g_msa[:, 0][:, None, :] * _mha(_mod(_ln(x0), sh_msa[:, 0], sc_msa[:, 0]), attn_qkv_w, attn_qkv_b, attn_proj_w, attn_proj_b)
        x1 = x1 + g_msa[:, 1][:, None, :] * _mha(_mod(_ln(x1), sh_msa[:, 1], sc_msa[:, 1]), attn_qkv_w, attn_qkv_b, attn_proj_w, attn_proj_b)
        xm = _mod(_ln(x0), sh_mca[:, 0], sc_mca[:, 0])
        ym = _mod(_ln(x1), sh_mca[:, 1], sc_mca[:, 1])
        qx, kx, vx = _heads(xm, crs_qkv_w, crs_qkv_b)
        qy, ky, vy = _heads(ym, crs_qkv_w, crs_qkv_b)
        ox = _attend(qx, ky, vy) @ crs_proj_w + crs_proj_b
        oy = _attend(qy, kx, vx) @ crs_proj_w + crs_proj_b
        x = x + jnp.concatenate((g_mca[:, 0][:, None, :] * ox, g_mca[:, 1][:, None, :] * oy), axis=1)

        def mlp(z):
            return jax.nn.gelu(z @ mlp_fc1_w + mlp_fc1_b, approximate=True) @ mlp_fc2_w + mlp_fc2_b
        m0 = mlp(_mod(_ln(x[:, :h]), sh_mlp[:, 0], sc_mlp[:, 0]))
        m1 = mlp(_mod(_ln(x[:, h:]), sh_mlp[:, 1], sc_mlp[:, 1]))
        x = x + jnp.concatenate((g_mlp[:, 0][:, None, :] * m0, g_mlp[:, 1][:, None, :] * m1), axis=1)
        return x

    def _L1_xattn_ref(tgt, memory, tgt_mask, sa_qw, sa_qb, sa_kw, sa_kb, sa_vw, sa_vb, sa_ow, sa_ob, ca_qw, ca_qb, ca_kw, ca_kb, ca_vw, ca_vb, ca_ow, ca_ob, w1, b1, w2, b2, g1, be1, g2, be2, g3, be3):
        import jax, jax.numpy as jnp
        import numpy as np
        D_MODEL = 256
        NHEAD = 16
        D_FF = 1024
        B = 2
        S = 512
        EPS = 1e-05

        def _mha(q_in, k_in, v_in, qw, qb, kw, kb, vw, vb, ow, ob, mask):
            b, sq, d = q_in.shape
            sk = k_in.shape[1]
            hd = d // NHEAD
            q = (q_in @ qw + qb).reshape(b, sq, NHEAD, hd).transpose(0, 2, 1, 3)
            k = (k_in @ kw + kb).reshape(b, sk, NHEAD, hd).transpose(0, 2, 1, 3)
            v = (v_in @ vw + vb).reshape(b, sk, NHEAD, hd).transpose(0, 2, 1, 3)
            scores = jnp.einsum('bhqd,bhkd->bhqk', q, k) / jnp.sqrt(jnp.float32(hd))
            if mask is not None:
                scores = jnp.where(mask == 0, jnp.float32(-1000000000.0), scores)
            attn = jax.nn.softmax(scores, axis=-1)
            out = jnp.einsum('bhqk,bhkd->bhqd', attn, v)
            out = out.transpose(0, 2, 1, 3).reshape(b, sq, d)
            return out @ ow + ob

        def _layernorm(x, g, b):
            mu = jnp.mean(x, axis=-1, keepdims=True)
            var = jnp.var(x, axis=-1, keepdims=True)
            return (x - mu) * jax.lax.rsqrt(var + EPS) * g + b
        x = tgt + _mha(tgt, tgt, tgt, sa_qw, sa_qb, sa_kw, sa_kb, sa_vw, sa_vb, sa_ow, sa_ob, tgt_mask)
        x = _layernorm(x, g1, be1)
        x = x + _mha(x, memory, memory, ca_qw, ca_qb, ca_kw, ca_kb, ca_vw, ca_vb, ca_ow, ca_ob, None)
        x = _layernorm(x, g2, be2)
        x = x + (jax.nn.relu(x @ w1 + b1) @ w2 + b2)
        x = _layernorm(x, g3, be3)
        return x
    x = _L0_xattn_ref(x, ctx_1024, L0_xattn_attn_qkv_w, L0_xattn_attn_qkv_b, L0_xattn_attn_proj_w, L0_xattn_attn_proj_b, L0_xattn_crs_qkv_w, L0_xattn_crs_qkv_b, L0_xattn_crs_proj_w, L0_xattn_crs_proj_b, L0_xattn_mlp_fc1_w, L0_xattn_mlp_fc1_b, L0_xattn_mlp_fc2_w, L0_xattn_mlp_fc2_b, L0_xattn_ada_w, L0_xattn_ada_b)
    x = _L1_xattn_ref(x, ctx_1024, mask_1x1xSxS_ik0, L1_xattn_sa_qw, L1_xattn_sa_qb, L1_xattn_sa_kw, L1_xattn_sa_kb, L1_xattn_sa_vw, L1_xattn_sa_vb, L1_xattn_sa_ow, L1_xattn_sa_ob, L1_xattn_ca_qw, L1_xattn_ca_qb, L1_xattn_ca_kw, L1_xattn_ca_kb, L1_xattn_ca_vw, L1_xattn_ca_vb, L1_xattn_ca_ow, L1_xattn_ca_ob, L1_xattn_w1, L1_xattn_b1, L1_xattn_w2, L1_xattn_b2, L1_xattn_g1, L1_xattn_be1, L1_xattn_g2, L1_xattn_be2, L1_xattn_g3, L1_xattn_be3)
    return x

_drawn_inputs = setup_inputs


def setup_inputs(seed=0):
    import zlib

    import numpy as np

    out = dict(_drawn_inputs(seed))
    spreads = {'L0_xattn_attn_qkv_b': (0.0, 0.8),
     'L0_xattn_attn_proj_b': (0.0, 0.8),
     'L0_xattn_crs_qkv_b': (0.0, 0.8),
     'L0_xattn_crs_proj_b': (0.0, 0.311),
     'L0_xattn_mlp_fc1_b': (0.0, 0.8),
     'L0_xattn_mlp_fc2_b': (0.0, 0.326),
     'L0_xattn_ada_b': (0.0, 0.412),
     'L1_xattn_sa_qb': (0.0, 0.8),
     'L1_xattn_sa_kb': (0.0, 2.0),
     'L1_xattn_sa_vb': (0.0, 0.946),
     'L1_xattn_sa_ob': (0.0, 0.306),
     'L1_xattn_ca_qb': (0.0, 0.8),
     'L1_xattn_ca_kb': (0.0, 2.0),
     'L1_xattn_ca_vb': (0.0, 0.1),
     'L1_xattn_ca_ob': (0.0, 0.1),
     'L1_xattn_b1': (0.0, 0.1),
     'L1_xattn_b2': (0.0, 0.1),
     'L1_xattn_g1': (1.0, 0.2),
     'L1_xattn_be1': (0.0, 0.1),
     'L1_xattn_g2': (1.0, 0.2),
     'L1_xattn_be2': (0.0, 0.1),
     'L1_xattn_g3': (1.0, 0.2),
     'L1_xattn_be3': (0.0, 0.1)}
    factors = {'L0_xattn_attn_qkv_w': 8.0,
     'L0_xattn_attn_proj_w': 8.0,
     'L0_xattn_crs_qkv_w': 8.0,
     'L0_xattn_crs_proj_w': 5.912,
     'L1_xattn_sa_qw': 8.0,
     'L1_xattn_sa_kw': 8.0,
     'L1_xattn_sa_vw': 8.0,
     'L1_xattn_ca_qw': 8.0,
     'L1_xattn_ca_kw': 8.0}
    for name, (base, spread) in spreads.items():
        noise = np.random.default_rng([zlib.crc32(name.encode()), seed]).standard_normal(out[name].shape)
        drawn = base * np.exp(spread * noise) if base else spread * noise
        out[name] = jnp.asarray(drawn.astype(out[name].dtype))
    for name, factor in factors.items():
        out[name] = (out[name] * factor).astype(out[name].dtype)
    return out
```

```python
from contextlib import ExitStack

import numpy as np
import concourse.bass as bass
from concourse import mybir

F32 = mybir.dt.float32
BF16 = mybir.dt.bfloat16
I32 = mybir.dt.int32
ALU = mybir.AluOpType
ACT = mybir.ActivationFunctionType
AX = mybir.AxisListType

P = 128
NT = 16
D = 256
H = 16
HD = 16
T = 2048
TC = 1601
CH = 512
QTERM = (0, 0, 0, 1, 1, 2)
KTERM = (0, 1, 2, 0, 1, 0)
KR = 100
MR = 97
NEG = -4.0e9
VW = 288


class Eng:

    def __init__(self, name, sem):
        self.name, self.sem, self.n, self.q, self.seen = name, sem, 0, [], {}

    def wait(self, *toks):
        for t in toks:
            if t is None:
                continue
            if isinstance(t, list):
                self.wait(*t)
                continue
            s, v = t
            if self.seen.get(s.name, 0) < v:
                self.seen[s.name] = v
                self.q.append(("w", s, v))

    def op(self, fn, *after, sig=True):
        self.wait(*after)
        if sig:
            self.n += 1
            self.q.append(("i", fn, self.sem, 1))
            return (self.sem, self.n)
        self.q.append(("i", fn, None, 0))
        return None

    def emit(self, eng):
        for it in self.q:
            if it[0] == "w":
                eng.wait_ge(it[1], it[2])
            else:
                r = it[1](eng)
                if it[2] is not None:
                    r.then_inc(it[2], it[3])


class Dma:

    def __init__(self, eng, sems):
        self.eng, self.sems, self.cnt, self.k = eng, sems, [0] * len(sems), 0

    def go(self, pairs, *after):
        k = self.k
        self.k = (k + 1) % len(self.sems)
        s = self.sems[k]
        self.eng.wait(*after)
        if self.cnt[k]:
            self.eng.wait((s, self.cnt[k]))
        for o, i in pairs:
            self.eng.q.append(("i", (lambda e, o=o, i=i: e.dma_start(o, i, allow_slow_non_contiguous=True)), s, 16))
            self.cnt[k] += 16
        return (s, self.cnt[k])

    def all_landed(self):
        for s, c in zip(self.sems, self.cnt):
            if c:
                self.eng.wait((s, c))


def xattn_kernel(nc, I, out):
    ctx = ExitStack()
    with ctx:
        def sb(name, shape, dt):
            return ctx.enter_context(nc.sbuf_tensor(name, shape, dt))

        def sem(name):
            return ctx.enter_context(nc.semaphore(name))

        def dram(name, shape, dt):
            return nc.dram_tensor(name, shape, dt, kind="Internal").ap()

        pe, act, dve, pool, sp = (Eng(n, sem("s_" + n)) for n in ("pe", "act", "dve", "pool", "sp"))
        q = Dma(sp, [sem(f"d{i}") for i in range(24)])

        ps = ctx.enter_context(nc.psum_tensor("ps", [P, 8, 512], F32))

        KS = sb("KS", [KR, H, T], BF16)
        QS = sb("QS", [KR, H, 2, CH], BF16)
        Vt = sb("Vt", [P, NT, VW], F32)
        x = sb("x", [P, NT, D], F32)
        PT = sb("PT", [P, 8, CH], F32)
        Oe = sb("Oe", [P, 2, CH], F32)
        ON = sb("ON", [P, 2, CH], F32)
        OD = sb("OD", [P, 2, CH], F32)
        XT = sb("XT", [P, 2, CH], F32)
        xn = sb("xn", [P, 4, D], F32)
        Qf = xn[:, :, :].rearrange("p (a b) n -> p a (b n)", a=2)
        S3 = sb("S3", [P, 3, 2, CH], BF16)
        wA = sb("wA", [P, 2, 768], F32)
        wP = sb("wP", [P, 2, D], F32)
        big = sb("big", [P, 6144], F32)
        identF = sb("identF", [P, P], F32)
        identB = sb("identB", [P, P], BF16)
        negI = sb("negI", [P, P], BF16)
        vb = sb("vb", [P, D], F32)
        GB = sb("GB", [P, 2, D], F32)
        G = sb("G", [P, 3, 2, D], F32)
        colb = sb("colb", [P, 12], F32)
        modT = sb("modT", [P, 18, 2], F32)
        st = sb("st", [P, 4, 6], F32)
        mv = sb("mv", [P, 4, 2], F32)
        rs = sb("rs", [P, 4], F32)
        mh = sb("mh", [P, 4], F32)
        mx = sb("mx", [P, 2, 16, 2], F32)
        nm = sb("nm", [P, 2, 16], F32)
        mr = sb("mr", [16, 2, 3, P], BF16)
        mf = sb("mf", [16, 2, P], F32)
        dd = sb("dd", [P, 2, 64], F32)

        w1 = big[:, 0:2048].rearrange("p (a n) -> p a n", a=2)
        w2 = big[:, 2048:4096].rearrange("p (a n) -> p a n", a=8)
        HT = big[:, 4096:6144].rearrange("p (a n) -> p a n", a=8)
        maskT = big[:, 0:4096].bitcast(BF16).rearrange("p (k n) -> p k n", k=NT)
        mstg = big[:, 4096:4608].bitcast(I32)
        mbf = big[:, 4608:4864].bitcast(BF16)
        keep = big[:, 4864:5120].bitcast(BF16)
        onesB = big[:, 5120:5184].bitcast(BF16)

        scr = [dram(f"scr{i}", [3, D, CH], BF16) for i in range(6)]
        scr_m = dram("scr_m", [4, 3, 4, CH], BF16)
        scr_d = dram("scr_d", [2, H, CH], F32)
        scr_r = dram("scr_r", [2, H, CH], F32)

        tok = {}

        def get(*keys):
            return [tok.get(k) for k in keys]

        def add(key, t):
            tok[key] = tok.get(key, []) + [t]

        m0 = pool.op(lambda e: e.memset(identF[:], 0.0))
        m1 = pool.op(lambda e: e.affine_select(out=identF[:], in_=identF[:], compare_op=ALU.not_equal, fill=1.0,
                                               base=0, pattern=[[-1, P]], channel_multiplier=1), m0)
        m2 = pool.op(lambda e: e.tensor_copy(identB[:], identF[:]), m1)
        m3 = pool.op(lambda e: e.tensor_scalar(negI[:], identF[:], NEG, None, ALU.mult), m1)
        m4 = pool.op(lambda e: e.memset(mh[:], -0.5), m3)
        ident = [m1, m2, m3, m4]
        k0 = dve.op(lambda e: e.memset(KS[96:100, :, :], 1.0))
        k1 = dve.op(lambda e: e.memset(KS[96:97, :, :], 0.0), k0)
        k2 = dve.op(lambda e: e.memset(QS[96:97, :, :, :], 1.0))
        k3 = dve.op(lambda e: e.memset(Vt[:], 1.0))
        consts = [k1, k2, k3]

        class Ring:
            def __init__(self, n):
                self.n, self.i, self.free = n, 0, [None] * n

            def take(self):
                s = self.i % self.n
                self.i += 1
                return s, self.free[s]

        M, A = Ring(2), Ring(3)

        def mslot(s):
            return ps[:, 3 + 2 * s:5 + 2 * s, :]

        def mflat(s):
            return mslot(s).rearrange("p a n -> p (a n)")

        def load_x(c, *after):
            tok["x", c] = [q.go([(x[:, 4 * c:4 * c + 4, :],
                                  I["x"][0, 512 * c:512 * c + 512, :].rearrange("(t p) d -> p t d", p=P))], *after)]

        for c in range(4):
            load_x(c)

        def load_cols(dst, vec):
            return (dst, vec.rearrange("(c p) -> p c", p=P))

        def load_w(dst, w):
            return (dst, w.rearrange("(a p) n -> p a n", p=P))

        ada = KS[:, :, :].rearrange("p h n -> p (h n)")
        adw = PT[:, :, :].rearrange("p a n -> p (a n)")
        cT = sb("cT", [P, 2, 2], F32)
        ce = sb("ce", [P, 2, 2], F32)
        adb = sb("adb", [P, 18], F32)
        cb = Oe[:, 0, :].rearrange("p (a r n) -> p a r n", a=2, r=2)
        t_c = q.go([(cT[:, a, r:r + 1], I["ctx_1024"][0, r, 128 * a:128 * a + 128].rearrange("(p o) -> p o", o=1))
                    for a in range(2) for r in range(2)] + [load_cols(adb[:], I["L0_xattn_ada_b"])])
        bb = ON[:, :, :].rearrange("p a n -> p (a n)")
        t_bb = q.go([(bb[:, 256 * g:256 * g + 256],
                      I["L0_xattn_ada_b"][768 * g + 512:768 * g + 768].partition_broadcast(P)) for g in range(3)])
        e1 = act.op(lambda e: e.activation(ce[:], cT[:], ACT.Exp, scale=-1.0), t_c)
        e2 = dve.op(lambda e: e.tensor_scalar(ce[:], ce[:], 1.0, None, ALU.add), e1)
        e3 = dve.op(lambda e: e.reciprocal(ce[:], ce[:]), e2)
        e4 = dve.op(lambda e: e.tensor_tensor(cT[:], cT[:], ce[:], ALU.mult), e3)
        e5 = dve.op(lambda e: e.tensor_copy(cb, cT[:].rearrange("p a (r o) -> p a r o", o=1)
                                            .to_broadcast([P, 2, 2, P])), e4)
        prev = None
        for g in range(3):
            src = I["L0_xattn_ada_w"][:, 768 * g:768 * g + 768].rearrange("(a p) n -> p a n", p=P)
            dst = adw[:, 0:1536] if g != 1 else adw[:, 1536:3072]
            dst = dst.rearrange("p (a n) -> p a n", a=2)
            tw = q.go([(dst, src)], prev if g == 2 else None)
            s, fr = M.take()
            mf_ = mflat(s)
            for j in range(6):
                for a in range(2):
                    t1 = pe.op(lambda e, j=j, a=a, mf_=mf_, dst=dst: e.matmul(
                        mf_[:, 2 * j:2 * j + 2], dst[:, a, 128 * j:128 * j + 128], cT[:, a, :],
                        start=a == 0, stop=a == 1), tw, e4, fr, sig=(j == 5 and a == 1))
            for r in range(2):
                for a in range(2):
                    t2 = pe.op(lambda e, r=r, a=a, mf_=mf_, dst=dst: e.matmul(
                        mf_[:, 512 + 256 * r:768 + 256 * r], cb[:, a, r, :], dst[:, a, 512:768],
                        start=a == 0, stop=a == 1), e5, sig=(r == 1 and a == 1))
            if g == 0:
                prev = t2
            u1 = dve.op(lambda e, g=g, mf_=mf_: e.tensor_tensor(
                modT[:, 6 * g:6 * g + 6, :], mf_[:, 0:12].rearrange("p (j r) -> p j r", r=2),
                adb[:, 6 * g:6 * g + 6].rearrange("p (j o) -> p j o", o=1).to_broadcast([P, 6, 2]), ALU.add), t1)
            u2 = dve.op(lambda e, g=g: e.tensor_scalar(modT[:, 6 * g + 2:6 * g + 4, :], modT[:, 6 * g + 2:6 * g + 4, :],
                                                       1.0, None, ALU.add), u1)
            for r in range(2):
                u3 = dve.op(lambda e, g=g, r=r, mf_=mf_: e.tensor_tensor(
                    G[:, g, r, :], mf_[:, 512 + 256 * r:768 + 256 * r], bb[:, 256 * g:256 * g + 256], ALU.add),
                    t2, t_bb)
            M.free[s] = u3
            tok["mod", g] = [u2, u3]
        tok["adw_free"] = [t2]
        tok["bb_free"] = [u3]

        def ln_stats(c, eps):
            for t in range(4):
                a = dve.op(lambda e, t=t: e.bn_stats(st[:, t, :], x[:, 4 * c + t, :]), get(("x", c)), sig=t == 3)
            for t in range(4):
                b = dve.op(lambda e, t=t: e.bn_aggr(mv[:, t, :], st[:, t, :]), a, get("mv_rd"), sig=t == 3)
            d = pool.op(lambda e: e.tensor_scalar(rs[:], mv[:, :, 1], eps, None, ALU.add), b, get("rs_rd"))
            f = pool.op(lambda e: e.tensor_tensor(rs[:], rs[:], mh[:], ALU.pow), d)
            tok["rs"] = [f]
            tok["mv_rd"] = [d]

        def ln_xn(c):
            for t in range(4):
                a = dve.op(lambda e, t=t: e.tensor_scalar(xn[:, t, :], x[:, 4 * c + t, :], mv[:, t, 0:1],
                                                          rs[:, t:t + 1], ALU.subtract, ALU.mult),
                           get("rs", "xn_rd"), sig=t == 3)
            tok["xn"] = [a]
            tok["rs_rd"] = [a]
            add(("x_rd", c), a)

        def transpose_in(src, n, wr, scale=None, shift=None):
            s, fr = M.take()
            for a in range(2):
                for t in range((n + 127) // 128):
                    w = min(128, n - 128 * t)
                    z = pe.op(lambda e, t=t, a=a, w=w: e.transpose(
                        mslot(s)[:, a, 128 * t:128 * t + w], src[0:w, t, 128 * a:128 * a + 128], identF[0:w, 0:w]),
                        wr, fr, ident)
            for a in range(2):
                if scale is None:
                    if a == 0:
                        v0 = act.op(lambda e: e.copy(XT[:, 0, 0:n], mslot(s)[:, 0, 0:n]), z, get("xt_rd"))
                    else:
                        v1 = dve.op(lambda e: e.tensor_copy(XT[:, 1, 0:n], mslot(s)[:, 1, 0:n]), z, get("xt_rd"))
                elif a == 0:
                    v0 = act.op(lambda e: e.activation(XT[:, 0, 0:n], mslot(s)[:, 0, 0:n], ACT.Identity,
                                                       bias=shift[0], scale=scale[0]), z, get("xt_rd"))
                else:
                    v1 = dve.op(lambda e: e.tensor_scalar(XT[:, 1, 0:n], mslot(s)[:, 1, 0:n], scale[1], shift[1],
                                                          ALU.mult, ALU.add), z, get("xt_rd"))
            M.free[s] = [v0, v1]
            tok["xt"] = [v0, v1]
            return z

        def ln_mod(c, g):
            r = c // 2
            ln_stats(c, 1e-6)
            ln_xn(c)
            z = transpose_in(xn, 512, get("xn", ("mod", g)),
                             [modT[:, 6 * g + 2 + a, r:r + 1] for a in range(2)],
                             [modT[:, 6 * g + a, r:r + 1] for a in range(2)])
            tok["xn_rd"] = [z]

        nscr = [0]

        def proj_split(n, woff, bcol, dst, wr, terms):
            s, fr = M.take()
            for oc in range(2):
                for a in range(2):
                    z = pe.op(lambda e, oc=oc, a=a: e.matmul(
                        mslot(s)[:, oc, 0:n], wA[:, a, woff + 128 * oc:woff + 128 * oc + 128], XT[:, a, 0:n],
                        start=a == 0, stop=a == 1), fr, get("xt", "wA"), sig=(oc == 1 and a == 1))
            tok["xt_rd"] = [z]
            tok["wA_rd"] = [z]
            for oc in range(2):
                f = act.op(lambda e, oc=oc: e.activation(Qf[:, oc, 0:n], mslot(s)[:, oc, 0:n], ACT.Identity,
                                                         bias=colb[:, bcol + oc:bcol + oc + 1]),
                           z, get("xn_rd", "colb"))
            M.free[s] = f
            tok["colb_rd"] = [f]
            h = dve.op(lambda e: e.tensor_copy(S3[:, 0, :, 0:n], Qf[:, :, 0:n]), f, get("s3_rd"))
            r1 = pool.op(lambda e: e.tensor_tensor(Qf[:, :, 0:n], Qf[:, :, 0:n], S3[:, 0, :, 0:n], ALU.subtract), h)
            m = pool.op(lambda e: e.tensor_copy(S3[:, 1, :, 0:n], Qf[:, :, 0:n]), r1)
            l = pool.op(lambda e: e.tensor_tensor(S3[:, 2, :, 0:n], Qf[:, :, 0:n], S3[:, 1, :, 0:n], ALU.subtract), m)
            tok["xn_rd"] = [l]
            k = nscr[0] % len(scr)
            nscr[0] += 1
            w = q.go([(scr[k][:, 128 * oc:128 * oc + 128, 0:n].rearrange("t p n -> p t n"), S3[:, :, oc, 0:n])
                      for oc in range(2)], h, m, l, get(("scr_rd", k)))
            tok["s3_rd"] = [w]
            rd = q.go([(dst(16 * r, 16 * r + 16), scr[k][t, :, 0:n].rearrange("(h d) n -> d h n", d=HD))
                       for r, t in enumerate(terms)], w, wr)
            tok["scr_rd", k] = [rd]
            return rd

        def proj_q(c, slot, woff=0):
            tok["qs", slot] = [proj_split(512, woff, 0, lambda lo, hi: QS[lo:hi, :, slot, :],
                                          get(("qs_rd", slot)), QTERM)]

        def proj_k(col, n, key, rd, woff=256):
            tok[key] = [proj_split(n, woff, 2, lambda lo, hi: KS[lo:hi, :, col:col + n], rd, KTERM)]

        def proj_v(kt0, n, key, rd, woff=512):
            s, fr = M.take()
            nt = (n + 127) // 128
            w = min(n, 128)
            for t in range(nt):
                for a in range(2):
                    z = pe.op(lambda e, t=t, a=a: e.matmul(
                        mflat(s)[0:w, 256 * t:256 * t + 256], XT[:, a, 128 * t:128 * t + w], wA[:, a, woff:woff + 256],
                        start=a == 0, stop=a == 1), fr, get("xt", "wA"), sig=(t == nt - 1 and a == 1))
            tok["xt_rd"] = [z]
            tok["wA_rd"] = [z]
            vv = Vt[0:w, kt0:kt0 + nt, 0:272].rearrange("p t (h d) -> p t h d", d=17)
            for t in range(nt):
                v = dve.op(lambda e, t=t: e.tensor_tensor(
                    vv[:, t, :, 0:16], mflat(s)[0:w, 256 * t:256 * t + 256].rearrange("p (h d) -> p h d", d=16),
                    vb[0:w, :].rearrange("p (h d) -> p h d", d=16), ALU.add), z, rd, get("vb"), consts, sig=t == nt - 1)
            M.free[s] = v
            tok["vb_rd"] = [v]
            tok[key] = [v]

        um = [0]
        uo = [0]

        def max_tasks(hg, qs, keys, masked, kdep):
            b = um[0] % 2
            um[0] += 1
            parts = []
            for lo in range(0, keys[1] - keys[0], 1024):
                parts.append((keys[0] + lo, min(keys[1], keys[0] + lo + 1024)))
            tasks = []
            last = {}
            for h in range(4):
                for tq in range(4):
                    for i, (lo, hi) in enumerate(parts):
                        def quantum(h=h, tq=tq, i=i, lo=lo, hi=hi):
                            s, fr = M.take()
                            hh = 4 * hg + h
                            for b0 in range(lo, hi, 512):
                                n = min(512, hi - b0)
                                pe.op(lambda e, b0=b0, n=n: e.matmul(
                                    mflat(s)[:, b0 - lo:b0 - lo + n],
                                    QS[0:MR, hh, qs, 128 * tq:128 * tq + 128], KS[0:MR, hh, b0:b0 + n],
                                    start=True, stop=not masked), fr, get(("qs", qs)), kdep, consts, sig=False)
                                if masked:
                                    for kk in range(n // 128):
                                        pe.op(lambda e, b0=b0, kk=kk: e.matmul(
                                            mflat(s)[:, b0 - lo + 128 * kk:b0 - lo + 128 * kk + 128],
                                            maskT[:, b0 // 128 + kk, 128 * tq:128 * tq + 128], negI[:],
                                            start=False, stop=kk == n // 128 - 1), get("maskT"), ident, sig=False)
                            it = pe.q[-1]
                            pe.n += 1
                            pe.q[-1] = ("i", it[1], pe.sem, 1)
                            z = (pe.sem, pe.n)
                            M.free[s] = dve.op(lambda e: e.tensor_reduce(
                                out=mx[:, b, 4 * h + tq, i:i + 1], in_=mflat(s)[:, 0:hi - lo], axis=AX.X, op=ALU.max),
                                z, get(("mx_rd", b)))
                            last["r"] = M.free[s]
                            last["z"] = z
                        tasks.append(quantum)

            def fin():
                np_ = len(parts)
                a = dve.op(lambda e: e.tensor_reduce(out=nm[:, b, :], in_=mx[:, b, :, 0:np_], axis=AX.X, op=ALU.max,
                                                     negate=True), last["r"], get(("nm_rd", b)))
                tok["mx_rd", b] = [a]
                s, fr = M.take()
                z = pe.op(lambda e: e.transpose(mflat(s)[0:16, 0:128], nm[:, b, :], identF[:]), a, fr, ident)
                tok["nm_rd", b] = [z]
                src = mflat(s)[0:16, 0:128]
                h1 = dve.op(lambda e: e.tensor_copy(mr[:, b, 0, :], src), z, get(("mr_rd", b)))
                f1 = dve.op(lambda e: e.tensor_tensor(mf[:, b, :], src, mr[:, b, 0, :], ALU.subtract), h1)
                M.free[s] = f1
                h2 = dve.op(lambda e: e.tensor_copy(mr[:, b, 1, :], mf[:, b, :]), f1)
                h3 = dve.op(lambda e: e.tensor_tensor(mr[:, b, 2, :], mf[:, b, :], mr[:, b, 1, :], ALU.subtract), h2)
                d4 = um[0] % 4
                w = q.go([(scr_m[d4].rearrange("t h (k c) -> (h k) t c", c=128), mr[:, b, :, :])],
                         h1, h2, h3, get(("scrm_rd", d4)))
                tok["mr_rd", b] = [w]
                rd = q.go([(QS[97:100, 4 * hg:4 * hg + 4, qs, :], scr_m[d4])], w, last["z"], get(("qs_rd", qs)))
                tok["scrm_rd", d4] = [rd]
                tok["m", hg, qs] = [rd]
            tasks.append(fin)
            return tasks

        def exp_steps(hg, qs, ob, kts, masked, kdep, vdep):
            steps = []
            state = {}

            def s_step(i, j):
                col, vt, n = kts[i]
                a, fr = A.take()
                hh = 4 * hg + j
                pslot = (i % 2) * 4 + j
                z = pe.op(lambda e: e.matmul(ps[0:n, a, :], KS[0:KR, hh, col:col + n], QS[0:KR, hh, qs, :],
                                             start=True, stop=not masked),
                          fr, get(("qs", qs), ("m", hg, qs)), kdep, consts, sig=not masked)
                if masked:
                    z = pe.op(lambda e: e.matmul(ps[0:n, a, :], negI[:], maskT[:, vt, :], start=False, stop=True),
                              get("maskT"), ident)
                x_ = act.op(lambda e: e.activation(PT[0:n, pslot, :], ps[0:n, a, :], ACT.Exp, scale=0.25),
                            z, get(("pt_rd", i % 2)))
                A.free[a] = x_
                state["x", i, j] = x_
                state["z"] = z

            def pv(i):
                col, vt, n = kts[i]
                for j in range(4):
                    hh = 4 * hg + j
                    pslot = (i % 2) * 4 + j
                    z = pe.op(lambda e, hh=hh, j=j, pslot=pslot: e.matmul(
                        ps[32 * j:32 * j + 32, 7, :], Vt[0:n, vt, 17 * hh:17 * hh + 32], PT[0:n, pslot, :],
                        start=i == 0, stop=i == len(kts) - 1, tile_position=(0, 32 * j)),
                        [state["x", i, j]], get("o_free"), vdep, sig=j == 3)
                tok["pt_rd", i % 2] = [z]
                state["pv"] = z

            for i in range(len(kts)):
                for j in range(4):
                    def f(i=i, j=j):
                        s_step(i, j)
                        if j == 3 and i > 0:
                            pv(i - 1)
                    steps.append(f)

            def end():
                pv(len(kts) - 1)
                b = uo[0] % 2
                uo[0] += 1
                e_ = dve.op(lambda e: e.tensor_copy(Oe[:, b, :], ps[:, 7, :]), state["pv"], get(("oe_rd", b)))
                tok["o_free"] = [e_]
                tok["qs_rd", qs] = [state["z"]]
                w1_ = q.go([(ON[64 * (hg % 2) + 16 * j:64 * (hg % 2) + 16 * j + 16, hg // 2, :],
                             Oe[32 * j:32 * j + 16, b, :]) for j in range(4)]
                           + [(scr_d[ob, 4 * hg:4 * hg + 4, :], Oe[16:128:32, b, :])],
                           e_, get("on_rd", ("scrd_rd", ob), "bb_free"))
                tok["oe_rd", b] = [w1_]
                add("on", w1_)
            steps.append(end)
            return steps

        def norm(ob):
            r = q.go([(dd[:, ob, :], scr_d[ob].rearrange("h (s c) -> (h s) c", c=64))], get("on", ("dd_rd", ob)))
            tok["scrd_rd", ob] = [r]
            a = dve.op(lambda e: e.reciprocal(dd[:, ob, :], dd[:, ob, :]), r)
            w = q.go([(scr_r[ob].rearrange("h (s c) -> (h s) c", c=64), dd[:, ob, :])], a, get(("scrr_rd", ob)))
            tok["dd_rd", ob] = [w]
            g = q.go([(OD[:, k, :], bass.AP(scr_r.tensor, scr_r[ob, 8 * k, 0:1].offset, [[CH, 8], [0, 16], [1, CH]]))
                      for k in range(2)], w, get("od_rd"))
            tok["scrr_rd", ob] = [g]
            m = pool.op(lambda e: e.tensor_tensor(OD[:], ON[:], OD[:], ALU.mult), g, get("on"))
            tok["ot"] = [m]
            tok["on_rd"] = [m]
            tok["on"] = []

        def residual_l0(c, s, z, g, lo=0, nt=4, more=None):
            r = c // 2
            t1 = dve.op(lambda e: e.tensor_tensor(
                xn[:, lo:lo + nt, :], mflat(s)[:, 0:256 * nt].rearrange("p (t n) -> p t n", n=256),
                G[:, g, r:r + 1, :].to_broadcast([P, nt, D]), ALU.mult), z, get("xn_rd", ("mod", g)))
            M.free[s] = t1
            xs = x[:, 4 * c + lo:4 * c + lo + nt, :]
            t2 = pool.op(lambda e: e.tensor_tensor(xs, xs, xn[:, lo:lo + nt, :], ALU.add), t1, get(("x", c), ("x_rd", c)))
            t3 = pool.op(lambda e: e.tensor_tensor(xs, xs, GB[:, r:r + 1, :].to_broadcast([P, nt, D]), ALU.add),
                         t2, get("gb"))
            tok["gb_rd"] = [t3]
            tok["xn_rd"] = [t2]
            add(("x", c), t3)

        def residual_l1(c, s, z, lo=0, nt=4):
            xs = x[:, 4 * c + lo:4 * c + lo + nt, :]
            t1 = dve.op(lambda e: e.tensor_tensor(
                xs, mflat(s)[:, 0:256 * nt].rearrange("p (t n) -> p t n", n=256), xs, ALU.add),
                z, get(("x", c), ("x_rd", c)))
            M.free[s] = t1
            t3 = pool.op(lambda e: e.tensor_tensor(xs, xs, GB[:, 0:1, :].to_broadcast([P, nt, D]), ALU.add),
                         t1, get("gb"))
            tok["gb_rd"] = [t3]
            add(("x", c), t3)

        def outproj(c, res):
            s, fr = M.take()
            for t in range(4):
                for a in range(2):
                    z = pe.op(lambda e, t=t, a=a: e.matmul(
                        mflat(s)[:, 256 * t:256 * t + 256], OD[:, a, 128 * t:128 * t + 128], wP[:, a, :],
                        start=a == 0, stop=a == 1), fr, get("ot", "wP"), sig=(t == 3 and a == 1))
            tok["od_rd"] = [z]
            tok["wP_rd"] = [z]
            res(c, s, z)

        def ln_l1(c, gl):
            ln_stats(c, 1e-5)
            for t in range(4):
                xs = x[:, 4 * c + t, :]
                a = dve.op(lambda e, t=t, xs=xs: e.tensor_scalar(xs, xs, mv[:, t, 0:1], rs[:, t:t + 1],
                                                                 ALU.subtract, ALU.mult), get("rs", ("x", c)), sig=t == 3)
            tok["rs_rd"] = [a]
            xs = x[:, 4 * c:4 * c + 4, :]
            b = pool.op(lambda e: e.tensor_tensor(xs, xs, G[:, gl, 0:1, :].to_broadcast([P, 4, D]), ALU.mult),
                        a, get("lnp"))
            d = pool.op(lambda e: e.tensor_tensor(xs, xs, G[:, gl, 1:2, :].to_broadcast([P, 4, D]), ALU.add), b)
            tok["x", c] = [d]

        def mlp_hid(c, fn, hf, hp):
            s, fr = M.take()
            for i in range(4):
                for a in range(2):
                    z = pe.op(lambda e, i=i, a=a: e.matmul(
                        mflat(s)[:, 256 * i:256 * i + 256],
                        w1[:, a, 128 * (4 * hp + i):128 * (4 * hp + i) + 128],
                        XT[:, a, 256 * hf:256 * hf + 256], start=a == 0, stop=a == 1),
                        fr, get("xt", "w1"), sig=(i == 3 and a == 1))
            tok["xt_rd"] = [z]
            for i in range(4):
                v = act.op(lambda e, i=i, hc=4 * hp + i: e.activation(
                    HT[:, hc, :], mflat(s)[:, 256 * i:256 * i + 256], fn, bias=colb[:, 4 + hc:5 + hc]),
                    z, get("ht_rd", "colb"), sig=i == 3)
            M.free[s] = v
            tok["colb_rd"] = [v]
            tok["ht", hp] = [v]

        def mlp_out(c, hf, res):
            s, fr = M.take()
            for t in range(2):
                for hc in range(8):
                    z = pe.op(lambda e, t=t, hc=hc: e.matmul(
                        mflat(s)[:, 256 * t:256 * t + 256], HT[:, hc, 128 * t:128 * t + 128], w2[:, hc, :],
                        start=hc == 0, stop=hc == 7), fr, get(("ht", 0), ("ht", 1), "w2"),
                        sig=(t == 1 and hc == 7))
            tok["ht_rd"] = [z]
            tok["w_rd"] = [z]
            res(c, s, z, lo=2 * hf, nt=2)

        def mlp_tasks(c, fn, res):
            return [lambda hf=hf, k=k: mlp_out(c, hf, res) if k == 2 else mlp_hid(c, fn, hf, k)
                    for hf in range(2) for k in range(3)]

        def mlp(c, fn, res):
            for f in mlp_tasks(c, fn, res):
                f()

        def run(fg, bg):
            n, done = len(fg) - 1, 0
            for i, f in enumerate(fg):
                f()
                want = min(i + 1, n) * len(bg) // n
                while done < want:
                    bg[done]()
                    done += 1

        def attention(units, kinfo, kts, masked, posts, before=None):
            todo = []
            seq = [(c, qs, hg) for c, qs in units for hg in range(4)]
            for f in max_tasks(seq[0][2], seq[0][1], kinfo(seq[0][0])[0], masked, kinfo(seq[0][0])[1]):
                f()
            for i, (c, qs, hg) in enumerate(seq):
                bg = []
                if i + 1 < len(seq):
                    c2, q2, h2 = seq[i + 1]
                    bg += max_tasks(h2, q2, kinfo(c2)[0], masked, kinfo(c2)[1])
                bg += todo
                todo = []
                kt_, vdep = kts(c)
                run(exp_steps(hg, qs, c % 2, kt_, masked, kinfo(c)[1], vdep), bg)
                if hg == 3:
                    todo = posts(c, qs)
            for f in todo:
                f()

        def load_layer(wlist, biases, vbias, proj, pbias):
            tok["wA"] = [q.go([load_w(wA[:, :, o:o + w.shape[1]], w) for o, w in wlist], get("wA_rd"))]
            tok["colb"] = [q.go([load_cols(colb[:, o:o + b.shape[0] // P], b) for o, b in biases], get("colb_rd"))]
            tok["vb"] = [q.go([(vb[:], vbias.partition_broadcast(P))], get("vb_rd"))]
            tok["wP"] = [q.go([load_w(wP[:], proj)], get("wP_rd"))]

        def gate_bias(g, b):
            a = q.go([(GB[:, 0, :], b.partition_broadcast(P)), (GB[:, 1, :], b.partition_broadcast(P))], get("gb_rd"))
            d = pool.op(lambda e: e.tensor_tensor(GB[:], GB[:], G[:, g, :, :], ALU.mult), a, get(("mod", g)))
            tok["gb"] = [d]

        for lay, (nm_, g) in enumerate((("attn", 0), ("crs", 1))):
            W = I[f"L0_xattn_{nm_}_qkv_w"]
            Bq = I[f"L0_xattn_{nm_}_qkv_b"]
            load_layer([(0, W)], [(0, Bq[0:512])], Bq[512:768], I[f"L0_xattn_{nm_}_proj_w"], None)
            gate_bias(g, I[f"L0_xattn_{nm_}_proj_b"])
            kr = get("ks_rd")
            for c in range(4):
                ln_mod(c, g)
                proj_k(512 * c, 512, ("k", c), kr)
                proj_v(4 * c, 512, ("v", c), kr)
                if c < 2:
                    proj_q(c, c)

            def kh(c, g=g):
                return (c // 2) ^ g

            def post(c, qs, g=g):
                def a():
                    if g == 1:
                        load_x(c, get(("x", c), ("x_rd", c)))
                    norm(c % 2)
                    outproj(c, lambda c, s, z: residual_l0(c, s, z, g))
                t = [a]
                if c < 2:
                    t = [lambda: ln_mod(c + 2, g), lambda: proj_q(c + 2, c)] + t
                return t

            attention([(0, 0), (1, 1), (2, 0), (3, 1)],
                      lambda c: ((1024 * kh(c), 1024 * kh(c) + 1024), get(("k", 2 * kh(c)), ("k", 2 * kh(c) + 1))),
                      lambda c: ([(1024 * kh(c) + 128 * i, 8 * kh(c) + i, 128) for i in range(8)],
                                 get(("v", 2 * kh(c)), ("v", 2 * kh(c) + 1))),
                      False, post)
            tok["ks_rd"] = [(pe.sem, pe.n)]

        tok["w1"] = [q.go([load_w(w1, I["L0_xattn_mlp_fc1_w"])])]
        tok["w2"] = [q.go([load_w(w2, I["L0_xattn_mlp_fc2_w"])])]
        tok["colb"] = [q.go([load_cols(colb[:, 4:12], I["L0_xattn_mlp_fc1_b"])], get("colb_rd"))]
        gate_bias(2, I["L0_xattn_mlp_fc2_b"])
        for c in range(4):
            ln_mod(c, 2)
            mlp(c, ACT.Gelu_apprx_tanh, lambda c, s, z, lo=0, nt=4: residual_l0(c, s, z, 2, lo, nt))

        tok["lnp"] = [q.go([(G[:, i, j, :], I[f"L1_xattn_{n}{i + 1}"].partition_broadcast(P))
                            for i in range(3) for j, n in enumerate(("g", "be"))],
                           get("xn_rd", "gb"), (dve.sem, dve.n), (pool.sem, pool.n))]

        def load_l1(p):
            load_layer([(0, I[f"L1_xattn_{p}_qw"]), (256, I[f"L1_xattn_{p}_kw"]), (512, I[f"L1_xattn_{p}_vw"])],
                       [(0, I[f"L1_xattn_{p}_qb"]), (2, I[f"L1_xattn_{p}_kb"])], I[f"L1_xattn_{p}_vb"],
                       I[f"L1_xattn_{p}_ow"], None)
            tok["gb"] = [q.go([(GB[:, 0, :], I[f"L1_xattn_{p}_ob"].partition_broadcast(P))], get("gb_rd"))]

        def x_to_xt(c):
            z = transpose_in(x[:, 4 * c:4 * c + 4, :], 512, get(("x", c)))
            tok["x_rd", c] = [z]

        load_l1("sa")
        kr = get("ks_rd")
        for c in range(4):
            x_to_xt(c)
            proj_k(512 * c, 512, ("k", c), kr)
            proj_v(4 * c, 512, ("v", c), kr)
        mask = I["mask_1x1xSxS_ik0"]
        ob_ = dve.op(lambda e: e.memset(onesB, 1.0), get("w_rd", "ht_rd"))

        def load_mask(c):
            w = [(pe.sem, pe.n)]
            for t in range(4):
                for kc in range(4):
                    l = q.go([(mstg, mask[0, 0, 512 * c + 128 * t:512 * c + 128 * t + 128, 512 * kc:512 * kc + 512])],
                             get("mstg_rd"), w, ob_)
                    v = dve.op(lambda e: e.tensor_scalar(mbf, mstg, 0.0, None, ALU.is_equal), l, get("mbf_rd"))
                    tok["mstg_rd"] = [v]
                    s, fr = M.take()
                    o = mslot(s)[:, 0, 0:256].bitcast(BF16).rearrange("p (k n) -> p k n", k=4)
                    for k in range(4):
                        z = pe.op(lambda e, k=k, o=o: e.transpose(o[:, k, :], mbf[:, 128 * k:128 * k + 128], identB[:]),
                                  v, fr, ident)
                    tok["mbf_rd"] = [z]
                    d = dve.op(lambda e, kc=kc, t=t, o=o: e.tensor_copy(
                        maskT[:, 4 * kc:4 * kc + 4, 128 * t:128 * t + 128], o), z, w)
                    M.free[s] = d
            s, fr = M.take()
            for k in range(NT):
                z = pe.op(lambda e, k=k, s=s: e.matmul(mslot(s)[:, 0, :], onesB, maskT[:, k, :],
                                                       start=k == 0, stop=k == NT - 1), d, fr, ob_, sig=k == NT - 1)
            kp = dve.op(lambda e: e.tensor_scalar(keep, mslot(s)[:, 0, :], float(T) - 0.5, None, ALU.is_lt), z)
            M.free[s] = kp
            mm = dve.op(lambda e: e.tensor_tensor(
                maskT, maskT, keep.rearrange("p (o n) -> p o n", o=1).to_broadcast([P, NT, CH]), ALU.mult), kp)
            tok["maskT"] = [mm]
            qq = dve.op(lambda e: e.tensor_tensor(
                QS[0:96, :, c % 2, :], QS[0:96, :, c % 2, :],
                keep[0:96, :].rearrange("p (o n) -> p o n", o=1).to_broadcast([96, H, CH]), ALU.mult),
                kp, get(("qs", c % 2)))
            tok["qs", c % 2] = [qq]

        def post1(c, qs):
            def a():
                norm(c % 2)
                outproj(c, residual_l1)
                ln_l1(c, 0)
            return [a]

        for c in range(4):
            x_to_xt(c)
            proj_q(c, c % 2)
            load_mask(c)
            attention([(c, c % 2)], lambda c: ((0, 2048), get(*[("k", i) for i in range(4)])),
                      lambda c: ([(128 * i, i, 128) for i in range(16)], get(*[("v", i) for i in range(4)])),
                      True, post1)
        tok["ks_rd"] = [(pe.sem, pe.n)]
        mask_done = (pe.sem, pe.n)

        load_l1("ca")
        kr = get("ks_rd")
        for c in range(4):
            n = min(512, TC - 512 * c)
            nt, w = (n + 127) // 128, min(n, 128)
            l = q.go([(xn[0:w, 0:nt, :], I["ctx_1024"][0, 512 * c:512 * c + n, :].rearrange("(t p) d -> p t d", p=w))],
                     get("xn_rd"))
            z = transpose_in(xn, n, l)
            tok["xn_rd"] = [z]
            proj_k(512 * c, n, ("k", c), kr)
            proj_v(4 * c, n, ("v", c), kr)

        def post2(c, qs):
            def a():
                norm(c % 2)
                outproj(c, residual_l1)
                ln_l1(c, 1)
            t = [a]
            if c < 2:
                t = [lambda: x_to_xt(c + 2), lambda: proj_q(c + 2, c)] + t
            return t

        for c in range(2):
            x_to_xt(c)
            proj_q(c, c)
        attention([(0, 0), (1, 1), (2, 0), (3, 1)],
                  lambda c: ((0, TC), get(*[("k", i) for i in range(4)])),
                  lambda c: ([(128 * i, i, min(128, TC - 128 * i)) for i in range(13)],
                             get(*[("v", i) for i in range(4)])),
                  False, post2)

        tok["w1"] = [q.go([load_w(w1, I["L1_xattn_w1"])], mask_done)]
        tok["w2"] = [q.go([load_w(w2, I["L1_xattn_w2"])], mask_done)]
        tok["colb"] = [q.go([load_cols(colb[:, 4:12], I["L1_xattn_b1"])], get("colb_rd"))]
        tok["gb"] = [q.go([(GB[:, 0, :], I["L1_xattn_b2"].partition_broadcast(P))], get("gb_rd"))]
        for c in range(4):
            x_to_xt(c)
            mlp(c, ACT.Relu, residual_l1)
            ln_l1(c, 2)
            q.go([(out[0, 512 * c:512 * c + 512, :].rearrange("(t p) d -> p t d", p=P), x[:, 4 * c:4 * c + 4, :])],
                 get(("x", c)))
        q.all_landed()

        block = ctx.enter_context(nc.Block())

        @block.sync
        def _(eng):
            sp.emit(eng)

        @block.gpsimd
        def _(eng):
            pool.emit(eng)

        @block.scalar
        def _(eng):
            act.emit(eng)

        @block.vector
        def _(eng):
            dve.emit(eng)

        @block.tensor
        def _(eng):
            pe.emit(eng)


_OUT = (1, 2048, 256)


def kernel(**inputs):
    import concourse.bacc as _bacc
    from concourse.bass_utils import run_bass_kernel_spmd as _run

    nc = _bacc.Bacc("TRN2", target_bir_lowering=False, num_devices=1, dynamic_dma_scratch_size=1024)
    arrays, aps = {}, {}
    for name, v in inputs.items():
        a = np.ascontiguousarray(v)
        arrays[f"in_{name}"] = a
        aps[name] = nc.dram_tensor(f"in_{name}", a.shape, mybir.dt.from_np(a.dtype), kind="ExternalInput").ap()
    o = nc.dram_tensor("out_0", _OUT, F32, kind="ExternalOutput").ap()
    xattn_kernel(nc, aps, o)
    r = _run(nc, [arrays], core_ids=[0])
    return r.results[0]["out_0"]
```

```python
from contextlib import ExitStack

import numpy as np
import concourse.bass as bass
from concourse import mybir

F32 = mybir.dt.float32
BF16 = mybir.dt.bfloat16
I32 = mybir.dt.int32
ALU = mybir.AluOpType
ACT = mybir.ActivationFunctionType
AX = mybir.AxisListType

P = 128
NT = 16
D = 256
H = 16
HD = 16
T = 2048
TC = 1601
CH = 512
QTERM = (0, 0, 0, 1, 1, 2)
KTERM = (0, 1, 2, 0, 1, 0)
TW = 2120
NKT = 17
KR = 100
MR = 97
NEG = -4.0e9
VW = 288
LEAD = 7


class Eng:

    def __init__(self, name, sem):
        self.name, self.sem, self.n, self.q, self.seen = name, sem, 0, [], {}

    def wait(self, *toks):
        for t in toks:
            if t is None:
                continue
            if isinstance(t, list):
                self.wait(*t)
                continue
            s, v = t
            if self.seen.get(s.name, 0) < v:
                self.seen[s.name] = v
                self.q.append(("w", s, v))

    def op(self, fn, *after, sig=True):
        self.wait(*after)
        if sig:
            self.n += 1
            self.q.append(("i", fn, self.sem, 1))
            return (self.sem, self.n)
        self.q.append(("i", fn, None, 0))
        return None

    def emit(self, eng, q=None):
        for it in self.q if q is None else q:
            if it[0] == "w":
                eng.wait_ge(it[1], it[2])
            elif it[0] == "b":
                r = eng.value_load(it[1], min_val=0, max_val=1)
                with eng.If(r > 0):
                    self.emit(eng, it[2])
                with eng.Else():
                    self.emit(eng, it[3])
            else:
                r = it[1](eng)
                if it[2] is not None:
                    r.then_inc(it[2], it[3])


class Dma:

    def __init__(self, eng, sems):
        self.eng, self.sems, self.cnt, self.k = eng, sems, [0] * len(sems), 0

    def go(self, pairs, *after):
        k = self.k
        self.k = (k + 1) % len(self.sems)
        s = self.sems[k]
        self.eng.wait(*after)
        if self.cnt[k]:
            self.eng.wait((s, self.cnt[k]))
        for o, i in pairs:
            self.eng.q.append(("i", (lambda e, o=o, i=i: e.dma_start(o, i, allow_slow_non_contiguous=True)), s, 16))
            self.cnt[k] += 16
        return (s, self.cnt[k])

    def all_landed(self):
        for s, c in zip(self.sems, self.cnt):
            if c:
                self.eng.wait((s, c))


def xattn_kernel(nc, I, out):
    ctx = ExitStack()
    with ctx:
        def sb(name, shape, dt):
            return ctx.enter_context(nc.sbuf_tensor(name, shape, dt))

        def sem(name):
            return ctx.enter_context(nc.semaphore(name))

        def dram(name, shape, dt):
            return nc.dram_tensor(name, shape, dt, kind="Internal").ap()

        pe, act, dve, pool, sp = (Eng(n, sem("s_" + n)) for n in ("pe", "act", "dve", "pool", "sp"))
        q = Dma(sp, [sem(f"d{i}") for i in range(24)])

        ps = ctx.enter_context(nc.psum_tensor("ps", [P, 8, 512], F32))

        KS = sb("KS", [KR, H, TW], BF16)
        QS = sb("QS", [KR, H, 2, CH], BF16)
        Vt = sb("Vt", [P, NKT, VW], F32)
        x = sb("x", [P, NT, D], F32)
        PT = sb("PT", [P, 8, CH], F32)
        Oe = sb("Oe", [P, 1, CH], F32)
        ON = sb("ON", [P, 2, CH], F32)
        OD = sb("OD", [P, 2, CH], F32)
        XT = sb("XT", [P, 2, CH], F32)
        xn = sb("xn", [P, 4, D], F32)
        Qf = xn[:, :, :].rearrange("p (a b) n -> p a (b n)", a=2)
        S3 = sb("S3", [P, 3, 2, CH], BF16)
        wA = sb("wA", [P, 2, 768], F32)
        wP = sb("wP", [P, 2, D], F32)
        big = sb("big", [P, 6144], F32)
        identF = sb("identF", [P, P], F32)
        identB = sb("identB", [P, P], BF16)
        negI = sb("negI", [P, P], BF16)
        vb = sb("vb", [P, D], F32)
        GBt = sb("GBt", [P, 2, 2, D], F32)
        G = sb("G", [P, 3, 2, D], F32)
        colb = sb("colb", [P, 32], F32)
        modT = sb("modT", [P, 18, 2], F32)
        st = sb("st", [P, 4, 6], F32)
        mv = sb("mv", [P, 4, 2], F32)
        rs = sb("rs", [P, 4], F32)
        mh = sb("mh", [P, 4], F32)
        mx = sb("mx", [P, 2, 16, 4], F32)
        nm = sb("nm", [P, 2, 16], F32)
        mr = sb("mr", [16, 2, 3, P], BF16)
        mf = sb("mf", [16, 2, P], F32)
        dd = sb("dd", [P, 2, 64], F32)

        w1 = big[:, 0:2048].rearrange("p (a n) -> p a n", a=2)
        w2 = big[:, 2048:4096].rearrange("p (a n) -> p a n", a=8)
        HT = big[:, 4096:6144].rearrange("p (a n) -> p a n", a=8)
        maskT = big[:, 0:4096].bitcast(BF16).rearrange("p (k n) -> p k n", k=NT)
        mstg = big[:, 4096:4608].bitcast(I32)
        mbf = big[:, 4608:4864].bitcast(BF16)
        keep = big[:, 4864:5120].bitcast(BF16)
        onesB = big[:, 5120:5184].bitcast(BF16)

        scr = [dram(f"scr{i}", [3, D, CH], BF16) for i in range(6)]
        scr_m = dram("scr_m", [4, 3, 4, CH], BF16)
        scr_d = dram("scr_d", [2, H, CH], F32)
        scr_r = dram("scr_r", [2, H, CH], F32)

        tok = {}

        def get(*keys):
            return [tok.get(k) for k in keys]

        def add(key, t):
            tok[key] = tok.get(key, []) + [t]

        m0 = pool.op(lambda e: e.memset(identF[:], 0.0))
        m1 = pool.op(lambda e: e.affine_select(out=identF[:], in_=identF[:], compare_op=ALU.not_equal, fill=1.0,
                                               base=0, pattern=[[-1, P]], channel_multiplier=1), m0)
        m2 = pool.op(lambda e: e.tensor_copy(identB[:], identF[:]), m1)
        m3 = pool.op(lambda e: e.tensor_scalar(negI[:], identF[:], NEG, None, ALU.mult), m1)
        m4 = pool.op(lambda e: e.memset(mh[:], -0.5), m3)
        ident = [m1, m2, m3, m4]
        k3 = dve.op(lambda e: e.memset(Vt[:], 1.0))
        k1 = pool.op(lambda e: e.memset(KS[96:100, :, :].bitcast(I32), 0x3F803F80), m4)
        k2 = pool.op(lambda e: e.memset(KS[96:97, :, :].bitcast(I32), 0), k1)
        k4 = pool.op(lambda e: e.memset(QS[96:97, :, :, :].bitcast(I32), 0x3F803F80), k2)
        consts = [k2, k3, k4]

        class Ring:
            def __init__(self, n):
                self.n, self.i, self.free = n, 0, [None] * n

            def take(self):
                s = self.i % self.n
                self.i += 1
                return s, self.free[s]

        M, A = Ring(2), Ring(3)

        def mslot(s):
            return ps[:, 3 + 2 * s:5 + 2 * s, :]

        def mflat(s):
            return mslot(s).rearrange("p a n -> p (a n)")

        def load_x(c, *after):
            tok["x", c] = [q.go([(x[:, 4 * c:4 * c + 4, :],
                                  I["x"][0, 512 * c:512 * c + 512, :].rearrange("(t p) d -> p t d", p=P))], *after)]


        def load_cols(dst, vec):
            return (dst, vec.rearrange("(c p) -> p c", p=P))

        def load_w(dst, w):
            return (dst, w.rearrange("(a p) n -> p a n", p=P))

        adw = PT[:, :, :].rearrange("p a n -> p (a n)")
        cT = sb("cT", [P, 2, 2], F32)
        ce = sb("ce", [P, 2, 2], F32)
        adb = sb("adb", [P, 18], F32)
        cb = Oe[:, 0, :].rearrange("p (a r n) -> p a r n", a=2, r=2)
        t_c = q.go([(cT[:, a, r:r + 1], I["ctx_1024"][0, r, 128 * a:128 * a + 128].rearrange("(p o) -> p o", o=1))
                    for a in range(2) for r in range(2)] + [load_cols(adb[:], I["L0_xattn_ada_b"])])
        bb = ON[:, :, :].rearrange("p a n -> p (a n)")
        t_bb = q.go([(bb[:, 256 * g:256 * g + 256],
                      I["L0_xattn_ada_b"][768 * g + 512:768 * g + 768].partition_broadcast(P)) for g in range(3)])
        e1 = act.op(lambda e: e.activation(ce[:], cT[:], ACT.Exp, scale=-1.0), t_c)
        e2 = dve.op(lambda e: e.tensor_scalar(ce[:], ce[:], 1.0, None, ALU.add), e1)
        e3 = dve.op(lambda e: e.reciprocal(ce[:], ce[:]), e2)
        e4 = dve.op(lambda e: e.tensor_tensor(cT[:], cT[:], ce[:], ALU.mult), e3)
        e5 = dve.op(lambda e: e.tensor_copy(cb, cT[:].rearrange("p a (r o) -> p a r o", o=1)
                                            .to_broadcast([P, 2, 2, P])), e4)
        def modulation(g):
            src = I["L0_xattn_ada_w"][:, 768 * g:768 * g + 768].rearrange("(a p) n -> p a n", p=P)
            dst = adw[:, 0:1536] if g != 1 else adw[:, 1536:3072]
            dst = dst.rearrange("p (a n) -> p a n", a=2)
            tw = q.go([(dst, src)], get("adw_rd") if g == 2 else None)
            s, fr = M.take()
            mf_ = mflat(s)
            for j in range(6):
                for a in range(2):
                    t1 = pe.op(lambda e, j=j, a=a, mf_=mf_, dst=dst: e.matmul(
                        mf_[:, 2 * j:2 * j + 2], dst[:, a, 128 * j:128 * j + 128], cT[:, a, :],
                        start=a == 0, stop=a == 1), tw, e4, fr, sig=(j == 5 and a == 1))
            for r in range(2):
                for a in range(2):
                    t2 = pe.op(lambda e, r=r, a=a, mf_=mf_, dst=dst: e.matmul(
                        mf_[:, 512 + 256 * r:768 + 256 * r], cb[:, a, r, :], dst[:, a, 512:768],
                        start=a == 0, stop=a == 1), e5, sig=(r == 1 and a == 1))
            if g == 0:
                tok["adw_rd"] = [t2]
            u1 = dve.op(lambda e, g=g, mf_=mf_: e.tensor_tensor(
                modT[:, 6 * g:6 * g + 6, :], mf_[:, 0:12].rearrange("p (j r) -> p j r", r=2),
                adb[:, 6 * g:6 * g + 6].rearrange("p (j o) -> p j o", o=1).to_broadcast([P, 6, 2]), ALU.add), t1)
            u2 = dve.op(lambda e, g=g: e.tensor_scalar(modT[:, 6 * g + 2:6 * g + 4, :], modT[:, 6 * g + 2:6 * g + 4, :],
                                                       1.0, None, ALU.add), u1)
            for r in range(2):
                u3 = dve.op(lambda e, g=g, r=r, mf_=mf_: e.tensor_tensor(
                    G[:, g, r, :], mf_[:, 512 + 256 * r:768 + 256 * r], bb[:, 256 * g:256 * g + 256], ALU.add),
                    t2, t_bb)
            M.free[s] = u3
            tok["mod", g] = [u2, u3]
            tok["bb_free"] = [u3]

        modulation(0)
        for c in range(4):
            load_x(c)

        def ln_stats(c, eps):
            for t in range(4):
                a = dve.op(lambda e, t=t: e.bn_stats(st[:, t, :], x[:, 4 * c + t, :]), get(("x", c)), sig=t == 3)
            for t in range(4):
                b = dve.op(lambda e, t=t: e.bn_aggr(mv[:, t, :], st[:, t, :]), a, get("mv_rd"), sig=t == 3)
            d = pool.op(lambda e: e.tensor_scalar(rs[:], mv[:, :, 1], eps, None, ALU.add), b, get("rs_rd"))
            f = pool.op(lambda e: e.tensor_tensor(rs[:], rs[:], mh[:], ALU.pow), d)
            tok["rs"] = [f]
            tok["mv_rd"] = [d]

        def ln_xn(c):
            for t in range(4):
                a = dve.op(lambda e, t=t: e.tensor_scalar(xn[:, t, :], x[:, 4 * c + t, :], mv[:, t, 0:1],
                                                          rs[:, t:t + 1], ALU.subtract, ALU.mult),
                           get("rs", "xn_rd"), sig=t == 3)
            tok["xn"] = [a]
            tok["rs_rd"] = [a]
            add(("x_rd", c), a)

        def transpose_in(src, n, wr, scale=None, shift=None):
            s, fr = M.take()
            for a in range(2):
                for t in range((n + 127) // 128):
                    w = min(128, n - 128 * t)
                    z = pe.op(lambda e, t=t, a=a, w=w: e.transpose(
                        mslot(s)[:, a, 128 * t:128 * t + w], src[0:w, t, 128 * a:128 * a + 128], identF[0:w, 0:w]),
                        wr, fr, ident)
            for a in range(2):
                if scale is None:
                    if a == 0:
                        v0 = act.op(lambda e: e.copy(XT[:, 0, 0:n], mslot(s)[:, 0, 0:n]), z, get("xt_rd"))
                    else:
                        v1 = dve.op(lambda e: e.tensor_copy(XT[:, 1, 0:n], mslot(s)[:, 1, 0:n]), z, get("xt_rd"))
                elif a == 0:
                    v0 = act.op(lambda e: e.activation(XT[:, 0, 0:n], mslot(s)[:, 0, 0:n], ACT.Identity,
                                                       bias=shift[0], scale=scale[0]), z, get("xt_rd"))
                else:
                    v1 = dve.op(lambda e: e.tensor_scalar(XT[:, 1, 0:n], mslot(s)[:, 1, 0:n], scale[1], shift[1],
                                                          ALU.mult, ALU.add), z, get("xt_rd"))
            M.free[s] = [v0, v1]
            tok["xt"] = [v0, v1]
            return z

        def mod_xt(c, g):
            r = c // 2
            z = transpose_in(xn, 512, get("xn", ("mod", g)),
                             [modT[:, 6 * g + 2 + a, r:r + 1] for a in range(2)],
                             [modT[:, 6 * g + a, r:r + 1] for a in range(2)])
            tok["xn_rd"] = [z]

        nscr = [0]

        def proj_split(n, woff, bcol, dst, wr, terms):
            s, fr = M.take()
            for oc in range(2):
                for a in range(2):
                    z = pe.op(lambda e, oc=oc, a=a: e.matmul(
                        mslot(s)[:, oc, 0:n], wA[:, a, woff + 128 * oc:woff + 128 * oc + 128], XT[:, a, 0:n],
                        start=a == 0, stop=a == 1), fr, get("xt", "wA"), sig=(oc == 1 and a == 1))
            tok["xt_rd"] = [z]
            tok["wA_rd"] = [z]
            for oc in range(2):
                f = act.op(lambda e, oc=oc: e.activation(Qf[:, oc, 0:n], mslot(s)[:, oc, 0:n], ACT.Identity,
                                                         bias=colb[:, bcol + oc:bcol + oc + 1]),
                           z, get("xn_rd", "colb"), sig=oc == 1)
            for oc in range(2):
                h = act.op(lambda e, oc=oc: e.activation(S3[:, 0, oc, 0:n], mslot(s)[:, oc, 0:n], ACT.Identity,
                                                         bias=colb[:, bcol + oc:bcol + oc + 1]),
                           get("s3_rd"), sig=oc == 1)
            M.free[s] = h
            r1 = pool.op(lambda e: e.tensor_tensor(Qf[:, :, 0:n], Qf[:, :, 0:n], S3[:, 0, :, 0:n], ALU.subtract), f, h)
            m = pool.op(lambda e: e.tensor_copy(S3[:, 1, :, 0:n], Qf[:, :, 0:n]), r1)
            l = pool.op(lambda e: e.tensor_tensor(S3[:, 2, :, 0:n], Qf[:, :, 0:n], S3[:, 1, :, 0:n], ALU.subtract), m)
            tok["xn_rd"] = [l]
            k = nscr[0] % len(scr)
            nscr[0] += 1
            w = q.go([(scr[k][:, 128 * oc:128 * oc + 128, 0:n].rearrange("t p n -> p t n"), S3[:, :, oc, 0:n])
                      for oc in range(2)], h, m, l, get(("scr_rd", k)))
            tok["s3_rd"] = [w]
            rd = q.go([(dst(16 * r), scr[k][t, :, 0:n].rearrange("(h d) n -> d h n", d=HD))
                       for r, t in enumerate(terms)], w, wr)
            tok["scr_rd", k] = [rd]
            return rd

        def proj_q(c, slot, bc):
            tok["qs", slot] = [proj_split(512, 0, bc, lambda lo: QS[lo:lo + 16, :, slot, :],
                                          get(("qs_rd", slot)), QTERM)]

        def proj_k(col, n, key, rd, bc):
            tok[key] = [proj_split(n, 256, bc + 2, lambda lo: KS[lo:lo + 16, :, col:col + n], rd, KTERM)]

        def proj_v(kt0, n, key, rd, woff=512):
            s, fr = M.take()
            nt = (n + 127) // 128
            w = min(n, 128)
            for t in range(nt):
                for a in range(2):
                    z = pe.op(lambda e, t=t, a=a: e.matmul(
                        mflat(s)[0:w, 256 * t:256 * t + 256], XT[:, a, 128 * t:128 * t + w], wA[:, a, woff:woff + 256],
                        start=a == 0, stop=a == 1), fr, get("xt", "wA"), sig=(t == nt - 1 and a == 1))
            tok["xt_rd"] = [z]
            tok["wA_rd"] = [z]
            vv = Vt[0:w, kt0:kt0 + nt, 0:272].rearrange("p t (h d) -> p t h d", d=17)
            for t in range(nt):
                v = dve.op(lambda e, t=t: e.tensor_tensor(
                    vv[:, t, :, 0:16], mflat(s)[0:w, 256 * t:256 * t + 256].rearrange("p (h d) -> p h d", d=16),
                    vb[0:w, :].rearrange("p (h d) -> p h d", d=16), ALU.add), z, rd, get("vb"), consts, sig=t == nt - 1)
            M.free[s] = v
            tok["vb_rd"] = [v]
            tok[key] = [v]

        um = [0]
        nm4 = [0]
        uo = [0]

        def max_tasks(hg, qs, keys, masked, kdep):
            b = um[0] % 2
            um[0] += 1
            parts = [(lo, min(keys[1], lo + 512)) for lo in range(keys[0], keys[1], 512)]
            tasks = []
            last = {}

            def quantum(pp, tq, i, lo, hi):
                s, fr = M.take()
                pr, n = 2 * hg + pp, hi - lo
                for u in range(2):
                    z = pe.op(lambda e, u=u: e.matmul(
                        mslot(s)[:, u, 0:n], QS[0:MR, 2 * pr + u, qs, 128 * tq:128 * tq + 128],
                        KS[0:MR, 2 * pr + u, lo:hi], start=True, stop=not masked),
                        fr, get(("qs", qs)), kdep, consts, sig=u == 1)
                for u in range(2 if masked else 0):
                    for kk in range(n // 128):
                        z = pe.op(lambda e, u=u, kk=kk: e.matmul(
                            mslot(s)[:, u, 128 * kk:128 * kk + 128],
                            maskT[:, lo // 128 + kk, 128 * tq:128 * tq + 128], negI[:],
                            start=False, stop=kk == n // 128 - 1), get("maskT"), ident,
                            sig=(u == 1 and kk == n // 128 - 1))
                o = mx[:, b, :, i].rearrange("p (h k) -> p h k", k=4)[:, 2 * pp:2 * pp + 2, tq:tq + 1]
                M.free[s] = dve.op(lambda e: e.tensor_reduce(
                    out=o, in_=mslot(s)[:, :, 0:n], axis=AX.X, op=ALU.max), z, get(("mx_rd", b)))
                last["r"] = M.free[s]
                last["z"] = z

            def narrow(pp, i, lo, hi):
                s, fr = M.take()
                pr, n = 2 * hg + pp, hi - lo
                for u in range(2):
                    for tq in range(4):
                        z = pe.op(lambda e, u=u, tq=tq: e.matmul(
                            mslot(s)[:, u, n * tq:n * tq + n], QS[0:MR, 2 * pr + u, qs, 128 * tq:128 * tq + 128],
                            KS[0:MR, 2 * pr + u, lo:hi], start=True, stop=True),
                            fr, get(("qs", qs)), kdep, consts, sig=(u == 1 and tq == 3))
                M.free[s] = dve.op(lambda e: e.tensor_reduce(
                    out=mx[:, b, :, i].rearrange("p (h k) -> p h k", k=4)[:, 2 * pp:2 * pp + 2, :],
                    in_=mslot(s)[:, :, 0:4 * n].rearrange("p u (k n) -> p u k n", n=n), axis=AX.X, op=ALU.max),
                    z, get(("mx_rd", b)))
                last["r"] = M.free[s]
                last["z"] = z

            for pp in range(2):
                for i, (lo, hi) in enumerate(parts):
                    if hi - lo < 128:
                        tasks.append(lambda a=(pp, i, lo, hi): narrow(*a))
                for tq in range(4):
                    for i, (lo, hi) in enumerate(parts):
                        if hi - lo >= 128:
                            tasks.append(lambda a=(pp, tq, i, lo, hi): quantum(*a))

            def fin_a():
                np_ = len(parts)
                last["a"] = a = dve.op(lambda e: e.tensor_reduce(out=nm[:, b, :], in_=mx[:, b, :, 0:np_], axis=AX.X, op=ALU.max,
                                                     negate=True), last["r"], get(("nm_rd", b)))
                tok["mx_rd", b] = [a]

            def fin_b():
                a = last["a"]
                s, fr = M.take()
                z = pe.op(lambda e: e.transpose(mflat(s)[0:16, 0:128], nm[:, b, :], identF[:]), a, fr, ident)
                tok["nm_rd", b] = [z]
                src = mflat(s)[0:16, 0:128]
                h1 = dve.op(lambda e: e.tensor_copy(mr[:, b, 0, :], src), z, get(("mr_rd", b)))
                f1 = dve.op(lambda e: e.tensor_tensor(mf[:, b, :], src, mr[:, b, 0, :], ALU.subtract), h1)
                M.free[s] = f1
                h2 = dve.op(lambda e: e.tensor_copy(mr[:, b, 1, :], mf[:, b, :]), f1)
                h3 = dve.op(lambda e: e.tensor_tensor(mr[:, b, 2, :], mf[:, b, :], mr[:, b, 1, :], ALU.subtract), h2)
                d4 = nm4[0] % 4
                nm4[0] += 1
                w = q.go([(scr_m[d4].rearrange("t h (k c) -> (h k) t c", c=128), mr[:, b, :, :])],
                         h1, h2, h3, get(("scrm_rd", d4)))
                tok["mr_rd", b] = [w]
                rd = q.go([(QS[97:100, 4 * hg:4 * hg + 4, qs, :], scr_m[d4])], w, last["z"], get(("qs_rd", qs)))
                tok["scrm_rd", d4] = [rd]
                tok["m", hg, qs] = [rd]
            return tasks + [fin_a, fin_b]

        def exp_steps(hg, qs, ob, kts, masked, kdep, vdep):
            steps = []
            state = {}

            def s_step(i, pp):
                col, vt, n = kts[i]
                pr = 2 * hg + pp
                (a0, f0), (a1, f1) = A.take(), A.take()
                bk = (a0, a1)
                for u in range(2):
                    state["s", u] = z = pe.op(lambda e, u=u: e.matmul(
                        ps[0:n, bk[u], :], KS[0:KR, 2 * pr + u, col:col + n], QS[0:KR, 2 * pr + u, qs, :],
                        start=True, stop=not masked),
                        (f0, f1)[u], get(("qs", qs), ("m", hg, qs)), kdep, consts)
                for u in range(2 if masked else 0):
                    z = pe.op(lambda e, u=u: e.matmul(ps[0:n, bk[u], :], negI[:], maskT[:, vt, :],
                                                      start=False, stop=True), get("maskT"), ident)
                    state["s", u] = z
                for u in range(2):
                    x_ = act.op(lambda e, u=u: e.activation(PT[0:n, (i % 2) * 4 + 2 * pp + u, :], ps[0:n, bk[u], :],
                                                            ACT.Exp, scale=0.25),
                                state["s", u], get(("pt_rd", i % 2)))
                    A.free[bk[u]] = x_
                    state["x", i, 2 * pp + u] = x_
                state["z"] = z

            def pv(i):
                col, vt, n = kts[i]
                for j in range(4):
                    z = pe.op(lambda e, j=j: e.matmul(
                        ps[32 * j:32 * j + 32, 7, :], Vt[0:n, vt, 17 * (4 * hg + j):17 * (4 * hg + j) + 32],
                        PT[0:n, (i % 2) * 4 + j, :],
                        start=i == 0, stop=i == len(kts) - 1, tile_position=(0, 32 * j)),
                        [state["x", i, j]], get("o_free"), vdep, sig=j == 3)
                tok["pt_rd", i % 2] = [z]
                state["pv"] = z

            for i in range(len(kts)):
                for pp in range(2):
                    def f(i=i, pp=pp):
                        s_step(i, pp)
                        if pp == 1 and i > 0:
                            pv(i - 1)
                    steps.append(f)

            def end():
                pv(len(kts) - 1)
                b = 0
                uo[0] += 1
                e_ = dve.op(lambda e: e.tensor_copy(Oe[:, b, :], ps[:, 7, :]), state["pv"], get(("oe_rd", b)))
                tok["o_free"] = [e_]
                tok["qs_rd", qs] = [state["z"]]
                w1_ = q.go([(ON[64 * (hg % 2) + 16 * j:64 * (hg % 2) + 16 * j + 16, hg // 2, :],
                             Oe[32 * j:32 * j + 16, b, :]) for j in range(4)]
                           + [(scr_d[ob, 4 * hg:4 * hg + 4, :], Oe[16:128:32, b, :])],
                           e_, get("on_rd", ("scrd_rd", ob), "bb_free"))
                tok["oe_rd", b] = [w1_]
                add("on", w1_)
            steps.append(end)
            return steps

        def norm(ob):
            hold = {}

            def na():
                hold["r"] = q.go([(dd[:, ob, :], scr_d[ob].rearrange("h (s c) -> (h s) c", c=64))],
                                 get("on", ("dd_rd", ob)))
                tok["scrd_rd", ob] = [hold["r"]]

            def nb():
                a = dve.op(lambda e: e.reciprocal(dd[:, ob, :], dd[:, ob, :]), hold["r"])
                w = q.go([(scr_r[ob].rearrange("h (s c) -> (h s) c", c=64), dd[:, ob, :])], a, get(("scrr_rd", ob)))
                tok["dd_rd", ob] = [w]
                hold["g"] = q.go([(OD[:, k, :], bass.AP(scr_r.tensor, scr_r[ob, 8 * k, 0:1].offset,
                                                        [[CH, 8], [0, 16], [1, CH]])) for k in range(2)],
                                 w, get("od_rd"))
                tok["scrr_rd", ob] = [hold["g"]]

            def nc_():
                m = pool.op(lambda e: e.tensor_tensor(OD[:], ON[:], OD[:], ALU.mult), hold["g"], get("on"))
                tok["ot"] = [m]
                tok["on_rd"] = [m]
                tok["on"] = []
            return [(0, na), (2, nb), (3, nc_)]

        def residual_l0(c, s, z, g, lo=0, nt=4):
            r, gbi = c // 2, g % 2
            t1 = dve.op(lambda e: e.tensor_tensor(
                xn[:, lo:lo + nt, :], mflat(s)[:, 0:256 * nt].rearrange("p (t n) -> p t n", n=256),
                G[:, g, r:r + 1, :].to_broadcast([P, nt, D]), ALU.mult), z, get("xn_rd", ("mod", g)))
            M.free[s] = t1
            xs = x[:, 4 * c + lo:4 * c + lo + nt, :]
            t2 = pool.op(lambda e: e.tensor_tensor(xs, xs, xn[:, lo:lo + nt, :], ALU.add), t1, get(("x", c), ("x_rd", c)))
            t3 = pool.op(lambda e: e.tensor_tensor(xs, xs, GBt[:, gbi, r:r + 1, :].to_broadcast([P, nt, D]), ALU.add),
                         t2, get(("gb", gbi)))
            tok["gb_rd", gbi] = [t3]
            tok["xn_rd"] = [t2]
            add(("x", c), t3)

        def residual_l1(c, s, z, gbi, lo=0, nt=4):
            xs = x[:, 4 * c + lo:4 * c + lo + nt, :]
            t1 = dve.op(lambda e: e.tensor_tensor(
                xs, mflat(s)[:, 0:256 * nt].rearrange("p (t n) -> p t n", n=256), xs, ALU.add),
                z, get(("x", c), ("x_rd", c)))
            M.free[s] = t1
            t3 = pool.op(lambda e: e.tensor_tensor(xs, xs, GBt[:, gbi, 0:1, :].to_broadcast([P, nt, D]), ALU.add),
                         t1, get(("gb", gbi)))
            tok["gb_rd", gbi] = [t3]
            add(("x", c), t3)

        def outproj(c, res):
            s, fr = M.take()
            for t in range(4):
                for a in range(2):
                    z = pe.op(lambda e, t=t, a=a: e.matmul(
                        mflat(s)[:, 256 * t:256 * t + 256], OD[:, a, 128 * t:128 * t + 128], wP[:, a, :],
                        start=a == 0, stop=a == 1), fr, get("ot", "wP"), sig=(t == 3 and a == 1))
            tok["od_rd"] = [z]
            tok["wP_rd"] = [z]
            res(c, s, z)

        def ln_l1(c, gl):
            def scale():
                for t in range(4):
                    xs = x[:, 4 * c + t, :]
                    a = dve.op(lambda e, t=t, xs=xs: e.tensor_scalar(
                        xs, xs, mv[:, t, 0:1], rs[:, t:t + 1], ALU.subtract, ALU.mult), get("rs", ("x", c)), sig=t == 3)
                tok["rs_rd"] = [a]
                xs = x[:, 4 * c:4 * c + 4, :]
                b = pool.op(lambda e: e.tensor_tensor(xs, xs, G[:, gl, 0:1, :].to_broadcast([P, 4, D]), ALU.mult),
                            a, get(("lnp", gl)))
                d = pool.op(lambda e: e.tensor_tensor(xs, xs, G[:, gl, 1:2, :].to_broadcast([P, 4, D]), ALU.add), b)
                tok["x", c] = [d]
            return [(2, lambda: ln_stats(c, 1e-5)), (1, scale)]

        def mlp_hid(c, fn, bc, hf, hp):
            s, fr = M.take()
            for i in range(4):
                for a in range(2):
                    z = pe.op(lambda e, i=i, a=a: e.matmul(
                        mflat(s)[:, 256 * i:256 * i + 256],
                        w1[:, a, 128 * (4 * hp + i):128 * (4 * hp + i) + 128],
                        XT[:, a, 256 * hf:256 * hf + 256], start=a == 0, stop=a == 1),
                        fr, get("xt", "w1"), sig=(i == 3 and a == 1))
            tok["xt_rd"] = [z]
            for i in range(4):
                v = act.op(lambda e, i=i, hc=4 * hp + i: e.activation(
                    HT[:, hc, :], mflat(s)[:, 256 * i:256 * i + 256], fn, bias=colb[:, bc + hc:bc + hc + 1]),
                    z, get("ht_rd", "colb"), sig=i == 3)
            M.free[s] = v
            tok["colb_rd"] = [v]
            tok["ht", hp] = [v]

        def mlp_out(c, hf, res):
            s, fr = M.take()
            for t in range(2):
                for hc in range(8):
                    z = pe.op(lambda e, t=t, hc=hc: e.matmul(
                        mflat(s)[:, 256 * t:256 * t + 256], HT[:, hc, 128 * t:128 * t + 128], w2[:, hc, :],
                        start=hc == 0, stop=hc == 7), fr, get(("ht", 0), ("ht", 1), "w2"),
                        sig=(t == 1 and hc == 7))
            tok["ht_rd"] = [z]
            tok["w_rd"] = [z]
            res(c, s, z, lo=2 * hf, nt=2)

        def mlp_chain(c, fn, bc, res):
            return [(2, lambda: mlp_hid(c, fn, bc, 0, 0)), (0, lambda: mlp_hid(c, fn, bc, 0, 1)),
                    (2, lambda: mlp_out(c, 0, res)),
                    (1, lambda: mlp_hid(c, fn, bc, 1, 0)), (0, lambda: mlp_hid(c, fn, bc, 1, 1)),
                    (2, lambda: mlp_out(c, 1, res))]

        urgent, lazy, cur, since, side = [], [], [], [0], []

        def bg_step(force=False):
            since[0] += 1
            while True:
                if not cur:
                    src = urgent or lazy
                    if not src:
                        return False
                    cur.extend(src.pop(0)[1])
                if cur[0][0] > since[0] and not force:
                    return False
                _, f = cur.pop(0)
                f()
                since[0] = 0
                if not (cur and cur[0][0] == 0):
                    return True

        def bg_until(k):
            while urgent or any(d <= k for d, _ in lazy) or (cur and k >= 0):
                bg_step(True)

        def drain(chain):
            for _, f in chain:
                f()

        def attention(seq, first=True, beyond=None):
            def start(n):
                ph, c, qs, hg = seq[n] if n < len(seq) else beyond
                return max_tasks(hg, qs, ph.keys(c), ph.masked, ph.kdep(c))

            total = len(seq) + (beyond is not None)
            if first:
                for f in start(0):
                    f()
            size = [2 * len(ph.kts(c)) for ph, c, _, _ in seq]
            begin = [sum(size[:i]) for i in range(len(seq))]
            opens = [0] + [max(begin[k - 1] + 1, begin[k - 1] + size[k - 1] - LEAD) for k in range(1, total)]
            k, left, m, step = 0, [], 0, 0
            for i, (ph, c, qs, hg) in enumerate(seq):
                fg = exp_steps(hg, qs, c % 2, ph.kts(c), ph.masked, ph.kdep(c), ph.vdep(c))
                for f in fg[:-1]:
                    f()
                    if not left and k + 1 < total and (k == 0 or step >= opens[k]):
                        k += 1
                        if (seq[k] if k < len(seq) else beyond)[3] == 0:
                            bg_until(unit0[0] + k)
                        left = start(k)
                        m = len(left)
                        lo = step
                        span = max(1, opens[k] - lo)
                    step += 1
                    if left:
                        want = m if step - lo >= span else -(-(step - lo) * m // span)
                        while m - len(left) < min(want, m):
                            left.pop(0)()
                    if side and step % 4 == 3:
                        side.pop(0)()
                    bg_step()
                if k == i + 1:
                    while left:
                        left.pop(0)()
                fg[-1]()
                if hg == 3:
                    u, l = ph.post(c, qs)
                    urgent.extend(u)
                    lazy.extend(l)
            unit0[0] += len(seq)

        unit0 = [0]

        tok["colb"] = [q.go([load_cols(colb[:, o:o + v.shape[0] // P], v) for o, v in (
            (0, I["L0_xattn_attn_qkv_b"][0:512]), (4, I["L0_xattn_crs_qkv_b"][0:512]),
            (8, I["L1_xattn_sa_qb"]), (10, I["L1_xattn_sa_kb"]), (12, I["L1_xattn_ca_qb"]), (14, I["L1_xattn_ca_kb"]),
            (16, I["L0_xattn_mlp_fc1_b"]), (24, I["L1_xattn_b1"]))])]

        def load_wA(wlist, vbias):
            tok["wA"] = [q.go([load_w(wA[:, :, o:o + w.shape[1]], w) for o, w in wlist], get("wA_rd"))]
            tok["vb"] = [q.go([(vb[:], vbias.partition_broadcast(P))], get("vb_rd"))]

        def load_wP(w):
            tok["wP"] = [q.go([load_w(wP[:], w)], get("wP_rd"))]

        def load_mlp(a, b, *after):
            tok["w1"] = [q.go([load_w(w1, a)], get("w_rd"), *after)]
            tok["w2"] = [q.go([load_w(w2, b)], get("w_rd"), *after)]

        def gate_bias(g, b):
            gbi = g % 2
            a = q.go([(GBt[:, gbi, r, :], b.partition_broadcast(P)) for r in range(2)], get(("gb_rd", gbi)))
            d = pool.op(lambda e: e.tensor_tensor(GBt[:, gbi], GBt[:, gbi], G[:, g, :, :], ALU.mult),
                        a, get(("mod", g)))
            tok["gb", gbi] = [d]

        def plain_bias(gbi, b):
            tok["gb", gbi] = [q.go([(GBt[:, gbi, 0, :], b.partition_broadcast(P))], get(("gb_rd", gbi)))]

        def load_lnp(i, *after):
            tok["lnp", i] = [q.go([(G[:, i, j, :], I[f"L1_xattn_{n}{i + 1}"].partition_broadcast(P))
                                   for j, n in enumerate(("g", "be"))], *after)]

        def l0_weights(nm_):
            load_wA([(0, I[f"L0_xattn_{nm_}_qkv_w"])], I[f"L0_xattn_{nm_}_qkv_b"][512:768])

        def l1_weights(p):
            load_wA([(0, I[f"L1_xattn_{p}_qw"]), (256, I[f"L1_xattn_{p}_kw"]), (512, I[f"L1_xattn_{p}_vw"])],
                    I[f"L1_xattn_{p}_vb"])

        def ln_mod(c, g):
            return [(3, lambda: ln_stats(c, 1e-6)), (1, lambda: ln_xn(c)), (2, lambda: mod_xt(c, g))]

        def kv_l0(c, g, slot=None):
            kr = get("ks_rd", ("half_rd", c // 2))
            return (ln_mod(c, g) + [(1, lambda: proj_k(512 * c, 512, ("k", c), kr, 4 * g)),
                                    (1, lambda: proj_v(4 * c, 512, ("v", c), kr))]
                    + ([(1, lambda: proj_q(c, slot, 4 * g))] if slot is not None else []))

        def q_l0(c, slot, g):
            return ln_mod(c, g) + [(1, lambda: proj_q(c, slot, 4 * g))]

        def x_to_xt(c):
            z = transpose_in(x[:, 4 * c:4 * c + 4, :], 512, get(("x", c)))
            tok["x_rd", c] = [z]

        def x_q(c, slot, bc):
            return [(4, lambda: x_to_xt(c)), (1, lambda: proj_q(c, slot, bc))]

        def out_l0(c, g):
            ch = norm(c % 2) + [(2, lambda: outproj(c, lambda c, s, z: residual_l0(c, s, z, g)))]
            if g == 1:
                ch = [(0, lambda: load_x(c, get(("x", c), ("x_rd", c))))] + ch
            return ch

        def out_l1(c, gbi, gl):
            return norm(c % 2) + [(2, lambda: outproj(c, lambda c, s, z: residual_l1(c, s, z, gbi)))] + ln_l1(c, gl)

        class Phase:
            def __init__(self, keys, kdep, kts, vdep, post, masked=False):
                self.keys, self.kdep, self.kts, self.vdep, self.post, self.masked = keys, kdep, kts, vdep, post, masked

        def phase_l0(g, post):
            def h(c):
                return (c // 2) ^ g
            return Phase(lambda c: (1024 * h(c), 1024 * h(c) + 1024),
                         lambda c: get(("k", 2 * h(c)), ("k", 2 * h(c) + 1)),
                         lambda c: [(1024 * h(c) + 128 * i, 8 * h(c) + i, 128) for i in range(8)],
                         lambda c: get(("v", 2 * h(c)), ("v", 2 * h(c) + 1)), post)

        def phase_ca(col0, vt0, post):
            return Phase(lambda c: (col0, col0 + TC), lambda c: get(*[("k", i) for i in range(4)]),
                         lambda c: [(col0 + 128 * i, vt0 + i, min(128, TC - 128 * i)) for i in range(13)],
                         lambda c: get(*[("v", i) for i in range(4)]), post)

        def units(ph, order):
            return [(ph, c, i % 2, hg) for i, c in enumerate(order) for hg in range(4)]

        def ctx_kv(c, col0, vt0, kr):
            n = min(512, TC - 512 * c)
            nt, w = (n + 127) // 128, min(n, 128)
            hold = {}

            def a():
                hold["l"] = q.go([(xn[0:w, 0:nt, :],
                                   I["ctx_1024"][0, 512 * c:512 * c + n, :].rearrange("(t p) d -> p t d", p=w))],
                                 get("xn_rd"))

            def b():
                z = transpose_in(xn, n, hold["l"])
                tok["xn_rd"] = [z]
            return [(0, a), (2, b), (1, lambda: proj_k(col0 + 512 * c, n, ("k", c), kr, 12)),
                    (1, lambda: proj_v(vt0 + 4 * c, n, ("v", c), kr))]

        def mlp0(c):
            return ln_mod(c, 2) + mlp_chain(
                c, ACT.Gelu_apprx_tanh, 16, lambda c, s, z, lo=0, nt=4: residual_l0(c, s, z, 2, lo, nt))

        def mlp1(c, gbi):
            def store():
                q.go([(out[0, 512 * c:512 * c + 512, :].rearrange("(t p) d -> p t d", p=P),
                       x[:, 4 * c:4 * c + 4, :])], get(("x", c)))
            return [(4, lambda: x_to_xt(c))] + mlp_chain(
                c, ACT.Relu, 24, lambda c, s, z, lo=0, nt=4: residual_l1(c, s, z, gbi, lo, nt)) + ln_l1(c, 2) + [
                    (0, store)]

        ms = [big[:, 2048 * i:2048 * i + 2048].bitcast(I32) for i in range(2)]
        mb = big[:, 4096:5120].bitcast(BF16)
        macc = big[:, 5120:6144].bitcast(BF16)
        ones1 = sb("ones1", [P, 1], BF16)
        zc = big[0:1, 0:512]
        zt = big[0:1, 512:1024]
        br = sb("br", [1, 512], BF16)
        fl = sb("fl", [1, 8], F32)
        flag = sb("flag", [1, 1], I32)
        mask = I["mask_1x1xSxS_ik0"]
        t_one = pool.op(lambda e: e.memset(ones1[:], 1.0), consts)

        def scan(t, k):
            if k == 0:
                tok["ms", t % 2] = [q.go([(ms[t % 2], mask[0, 0, 128 * t:128 * t + 128, :])], get(("ms_rd", t % 2)))]
            src = ms[t % 2][:, 512 * k:512 * k + 512]
            dst = (macc if t == 0 else mb)[:, 512 * k:512 * k + 512]
            ac = macc[:, 512 * k:512 * k + 512]
            a = pool.op(lambda e: e.tensor_scalar(dst, src, 0.0, None, ALU.is_equal), get(("ms", t % 2), ("macc", k)))
            if k == 3:
                tok["ms_rd", t % 2] = [a]
            if t:
                a = pool.op(lambda e: e.tensor_tensor(ac, ac, dst, ALU.add), a)
            tok["macc", k] = [a]

        def judge():
            sums = []
            for i in range(2):
                s, fr = M.take()
                for j in range(2):
                    z = pe.op(lambda e, i=i, j=j, s=s: e.matmul(
                        mslot(s)[0:1, j, :], ones1[:], macc[:, 1024 * i + 512 * j:1024 * i + 512 * j + 512],
                        start=True, stop=True), [get(("macc", k)) for k in range(4)], fr, t_one, sig=j == 1)
                if i == 0:
                    d = dve.op(lambda e, s=s: e.tensor_reduce(out=fl[:, 0:1], in_=mflat(s)[0:1, :], axis=AX.X,
                                                              op=ALU.add), z)
                else:
                    d1 = dve.op(lambda e, s=s: e.tensor_reduce(out=fl[:, 1:2], in_=mslot(s)[0:1, 0, :], axis=AX.X,
                                                               op=ALU.add), z)
                    d = dve.op(lambda e, s=s: e.tensor_copy(zc, mslot(s)[0:1, 1, :]), z)
                M.free[s] = d
            tok["w_rd"] = [z]
            n = float(T)
            b = dve.op(lambda e: e.tensor_scalar(br[:], zc, n - 0.5, NEG, ALU.is_gt, ALU.mult), d)
            c = dve.op(lambda e: e.tensor_scalar(zt, zc, -n, None, ALU.add), d)
            c = dve.op(lambda e: e.tensor_tensor(zt, zt, zc, ALU.mult), c)
            c = dve.op(lambda e: e.tensor_reduce(out=fl[:, 2:3], in_=zt, axis=AX.X, op=ALU.add), c)
            f = dve.op(lambda e: e.tensor_reduce(out=fl[:, 3:4], in_=zc, axis=AX.X, op=ALU.add), c)
            g = dve.op(lambda e: e.tensor_tensor(fl[:, 0:1], fl[:, 0:1], fl[:, 1:2], ALU.add), f, d1)
            g = dve.op(lambda e: e.tensor_scalar(fl[:, 4:5], fl[:, 0:1], 1536 * n - 0.5, None, ALU.is_gt), g)
            g = dve.op(lambda e: e.tensor_scalar(fl[:, 5:6], fl[:, 2:3], -0.5, None, ALU.is_gt), g)
            g = dve.op(lambda e: e.tensor_scalar(fl[:, 6:7], fl[:, 3:4], 512 * n - 0.5, None, ALU.is_lt), g)
            g = dve.op(lambda e: e.tensor_tensor(fl[:, 4:5], fl[:, 4:5], fl[:, 5:6], ALU.mult), g)
            g = dve.op(lambda e: e.tensor_tensor(flag[:], fl[:, 4:5], fl[:, 6:7], ALU.mult), g)
            tok["flag"] = [g]
            tok["br"] = [b]

        l0_weights("attn")
        for c in range(2):
            drain(kv_l0(c, 0, c))
            modulation(c + 1)
        load_wP(I["L0_xattn_attn_proj_w"])
        gate_bias(0, I["L0_xattn_attn_proj_b"])

        def post0(c, qs):
            if c == 0:
                return [out_l0(0, 0), q_l0(2, 0, 0)], []
            if c == 1:
                tok["half_rd", 0] = [(pe.sem, pe.n)]
                return [out_l0(1, 0), q_l0(3, 1, 0) + [(0, lambda: l0_weights("crs"))]], [
                    (99, kv_l0(0, 1)), (99, kv_l0(1, 1))]
            if c == 2:
                return [out_l0(2, 0), q_l0(2, 0, 1)], []
            return [], []

        def chains(f):
            def g(c, qs):
                u, l = f(c, qs)
                return [(0, x_) for x_ in u], l
            return g

        lazy.extend([(8, kv_l0(2, 0)), (8, kv_l0(3, 0))])
        side.extend([lambda t=t, k=k: scan(t, k) for t in range(NT) for k in range(4)])
        ph0 = phase_l0(0, chains(post0))
        ph1 = phase_l0(1, None)
        attention(units(ph0, (0, 1, 2, 3)), beyond=(ph1, 2, 0, 0))
        bg_until(999)
        for f in side:
            f()
        side.clear()
        tok["half_rd", 1] = [(pe.sem, pe.n)]
        judge()
        base = unit0[0]

        def fast():
            half0, half1 = get(("half_rd", 0)), []

            def crs_start():
                load_wP(I["L0_xattn_crs_proj_w"])
                gate_bias(1, I["L0_xattn_crs_proj_b"])
                load_mlp(I["L0_xattn_mlp_fc1_w"], I["L0_xattn_mlp_fc2_w"])
            urgent.extend([(0, out_l0(3, 0) + [(0, crs_start)]), (0, kv_l0(3, 1, 1)), (0, kv_l0(2, 1))])

            def sa_kv():
                def weights():
                    l1_weights("sa")
                    load_lnp(0, get("xn_rd"), (pool.sem, pool.n), (dve.sem, dve.n))
                kr = [(pe.sem, pe.n)]

                def row():
                    bi = q.go([(KS[96:97, :, 0:512],
                                br[:].rearrange("a (p n) -> a p n", p=1).to_broadcast([1, H, 512]))], get("br"), kr)
                    tok["sak"] = get(("k", 0)) + [bi]
                return [(0, weights), (4, lambda: x_to_xt(3)), (1, lambda: proj_k(0, 512, ("k", 0), kr, 8)), (0, row),
                        (1, lambda: proj_v(0, 512, "sav", kr))]

            def post(c, qs):
                if c == 2:
                    return [out_l0(2, 1) + [(0, lambda: gate_bias(2, I["L0_xattn_mlp_fc2_b"]))], q_l0(0, 0, 1)], [
                        (99, mlp0(2))]
                if c == 3:
                    return [out_l0(3, 1), q_l0(1, 1, 1)], [(99, mlp0(3)), (99, sa_kv())]
                if c == 0:
                    return [out_l0(0, 1)], [(base + 16, x_q(2, 0, 8)), (99, mlp0(0))]
                half1.append((pe.sem, pe.n))
                return [out_l0(1, 1) + [(0, sa_start)]], [(base + 20, x_q(3, 1, 8)), (99, mlp0(1))]

            def sa_start():
                load_wP(I["L1_xattn_sa_ow"])
                plain_bias(1, I["L1_xattn_sa_ob"])

            def post_sa(c, qs):
                if c == 2:
                    return [out_l1(2, 1, 0)], [(base + 24, x_q(0, 0, 8))]
                if c == 3:
                    return [out_l1(3, 1, 0)], [(base + 28, x_q(1, 1, 8) + [(0, lambda: l1_weights("ca"))])] + [
                        (base + 32, ctx_kv(k, 512, 4, half1)) for k in range(2)]
                if c == 0:
                    return [out_l1(0, 1, 0)], [(base + 32, ctx_kv(k, 512, 4, half1)) for k in range(2, 4)] + [
                        (base + 32, x_q(2, 0, 12))]
                return [out_l1(1, 1, 0) + [(0, ca_start)]], [(base + 36, x_q(3, 1, 12))]

            def ca_start():
                load_wP(I["L1_xattn_ca_ow"])
                plain_bias(0, I["L1_xattn_ca_ob"])
                load_lnp(1, (pool.sem, pool.n), (dve.sem, dve.n))
                load_lnp(2, (pool.sem, pool.n), (dve.sem, dve.n))
                load_mlp(I["L1_xattn_w1"], I["L1_xattn_w2"])

            def post_ca(c, qs):
                if c == 2:
                    return [out_l1(2, 0, 1) + [(0, lambda: plain_bias(1, I["L1_xattn_b2"]))], x_q(0, 0, 12)], [
                        (99, mlp1(2, 1))]
                if c == 3:
                    return [out_l1(3, 0, 1), x_q(1, 1, 12)], [(99, mlp1(3, 1))]
                return [out_l1(c, 0, 1)], [(99, mlp1(c, 1))]

            p1, p3 = phase_l0(1, chains(post)), phase_ca(512, 4, chains(post_ca))
            p2 = Phase(lambda c: (0, 512), lambda c: tok["sak"], lambda c: [(128 * i, i, 128) for i in range(4)],
                       lambda c: tok["sav"], chains(post_sa))
            order = (2, 3, 0, 1)
            attention(units(p1, order) + units(p2, order) + units(p3, order), first=False)
            bg_until(999)

        def load_mask(c):
            w = [(pe.sem, pe.n)]
            ob_ = dve.op(lambda e: e.memset(onesB, 1.0), w)
            for t in range(4):
                for kc in range(4):
                    l = q.go([(mstg, mask[0, 0, 512 * c + 128 * t:512 * c + 128 * t + 128, 512 * kc:512 * kc + 512])],
                             get("mstg_rd"), w, ob_)
                    v = dve.op(lambda e: e.tensor_scalar(mbf, mstg, 0.0, None, ALU.is_equal), l, get("mbf_rd"))
                    tok["mstg_rd"] = [v]
                    s, fr = M.take()
                    o = mslot(s)[:, 0, 0:256].bitcast(BF16).rearrange("p (k n) -> p k n", k=4)
                    for k in range(4):
                        z = pe.op(lambda e, k=k, o=o: e.transpose(o[:, k, :], mbf[:, 128 * k:128 * k + 128], identB[:]),
                                  v, fr, ident)
                    tok["mbf_rd"] = [z]
                    d = dve.op(lambda e, kc=kc, t=t, o=o: e.tensor_copy(
                        maskT[:, 4 * kc:4 * kc + 4, 128 * t:128 * t + 128], o), z, w)
                    M.free[s] = d
            s, fr = M.take()
            for k in range(NT):
                z = pe.op(lambda e, k=k: e.matmul(mslot(s)[:, 0, :], onesB, maskT[:, k, :],
                                                  start=k == 0, stop=k == NT - 1), d, fr, ob_, sig=k == NT - 1)
            kp = dve.op(lambda e: e.tensor_scalar(keep, mslot(s)[:, 0, :], float(T) - 0.5, None, ALU.is_lt), z)
            M.free[s] = kp
            mm = dve.op(lambda e: e.tensor_tensor(
                maskT, maskT, keep.rearrange("p (o n) -> p o n", o=1).to_broadcast([P, NT, CH]), ALU.mult), kp)
            tok["maskT"] = [mm]
            t = dve.op(lambda e: e.tensor_tensor(
                QS[0:96, :, c % 2, :], QS[0:96, :, c % 2, :],
                keep[0:96, :].rearrange("p (o n) -> p o n", o=1).to_broadcast([96, H, CH]), ALU.mult),
                kp, get(("qs", c % 2)))
            tok["qs", c % 2] = [t]

        def general():
            none = lambda c, qs: ([], [])
            drain(out_l0(3, 0))
            load_wP(I["L0_xattn_crs_proj_w"])
            gate_bias(1, I["L0_xattn_crs_proj_b"])
            drain(kv_l0(2, 1) + kv_l0(3, 1, 1))

            def post(c, qs):
                return [(0, out_l0(c, 1))] + ([(0, q_l0(c - 2, qs, 1))] if c > 1 else []), []
            attention(units(phase_l0(1, post), (2, 3, 0, 1)), first=False)
            bg_until(999)
            tok["ks_rd"] = [(pe.sem, pe.n)]
            load_mlp(I["L0_xattn_mlp_fc1_w"], I["L0_xattn_mlp_fc2_w"])
            gate_bias(2, I["L0_xattn_mlp_fc2_b"])
            for c in range(4):
                drain(mlp0(c))
            for i in range(3):
                load_lnp(i, get("xn_rd"), (dve.sem, dve.n), (pool.sem, pool.n))
            l1_weights("sa")
            load_wP(I["L1_xattn_sa_ow"])
            plain_bias(1, I["L1_xattn_sa_ob"])
            kr = get("ks_rd")
            for c in range(4):
                x_to_xt(c)
                proj_k(512 * c, 512, ("k", c), kr, 8)
                proj_v(4 * c, 512, ("v", c), kr)
            p2 = Phase(lambda c: (0, T), lambda c: get(*[("k", i) for i in range(4)]),
                       lambda c: [(128 * i, i, 128) for i in range(16)], lambda c: get(*[("v", i) for i in range(4)]),
                       none, True)
            for c in range(4):
                drain(x_q(c, c % 2, 8))
                load_mask(c)
                attention([(p2, c, c % 2, hg) for hg in range(4)])
                drain(out_l1(c, 1, 0))
            kr = [(pe.sem, pe.n)]
            l1_weights("ca")
            load_wP(I["L1_xattn_ca_ow"])
            plain_bias(0, I["L1_xattn_ca_ob"])
            plain_bias(1, I["L1_xattn_b2"])
            load_mlp(I["L1_xattn_w1"], I["L1_xattn_w2"], kr, (dve.sem, dve.n))
            for c in range(4):
                drain(ctx_kv(c, 0, 0, kr))
            p3 = phase_ca(0, 0, none)
            for c in range(4):
                drain(x_q(c, c % 2, 12))
                attention([(p3, c, c % 2, hg) for hg in range(4)])
                drain(out_l1(c, 0, 1))
                drain(mlp1(c, 1))

        engs = (pe, act, dve, pool, sp)
        for e in engs:
            e.wait(get("flag"))
        state0 = ([(e.n, dict(e.seen)) for e in engs], (list(q.cnt), q.k), dict(tok), (M.i, list(M.free)),
                  (A.i, list(A.free)), (um[0], uo[0], nm4[0], nscr[0], unit0[0]))
        arms = []
        for arm in (fast, general):
            es, qst, tk, mst, ast, cn = state0
            main = [e.q for e in engs]
            for e, (n, seen) in zip(engs, es):
                e.n, e.seen, e.q = n, dict(seen), []
            q.cnt, q.k = list(qst[0]), qst[1]
            tok.clear()
            tok.update(tk)
            M.i, M.free, A.i, A.free = mst[0], list(mst[1]), ast[0], list(ast[1])
            um[0], uo[0], nm4[0], nscr[0], unit0[0] = cn
            arm()
            q.all_landed()
            arms.append([e.q for e in engs])
            for e, old in zip(engs, main):
                e.q = old
        for e, a, b in zip(engs, *arms):
            e.q.append(("b", flag[0:1, 0:1], a, b))

        block = ctx.enter_context(nc.Block())

        @block.sync
        def _(eng):
            sp.emit(eng)

        @block.gpsimd
        def _(eng):
            pool.emit(eng)

        @block.scalar
        def _(eng):
            act.emit(eng)

        @block.vector
        def _(eng):
            dve.emit(eng)

        @block.tensor
        def _(eng):
            pe.emit(eng)


_OUT = (1, 2048, 256)


def kernel(**inputs):
    import concourse.bacc as _bacc
    from concourse.bass_utils import run_bass_kernel_spmd as _run

    nc = _bacc.Bacc("TRN2", target_bir_lowering=False, num_devices=1, dynamic_dma_scratch_size=1024)
    arrays, aps = {}, {}
    for name, v in inputs.items():
        a = np.ascontiguousarray(v)
        arrays[f"in_{name}"] = a
        aps[name] = nc.dram_tensor(f"in_{name}", a.shape, mybir.dt.from_np(a.dtype), kind="ExternalInput").ap()
    o = nc.dram_tensor("out_0", _OUT, F32, kind="ExternalOutput").ap()
    xattn_kernel(nc, aps, o)
    r = _run(nc, [arrays], core_ids=[0])
    return r.results[0]["out_0"]
```

```python
from contextlib import ExitStack

import numpy as np
import concourse.bass as bass
from concourse import mybir

F32 = mybir.dt.float32
BF16 = mybir.dt.bfloat16
I32 = mybir.dt.int32
ALU = mybir.AluOpType
ACT = mybir.ActivationFunctionType
AX = mybir.AxisListType

P = 128
NT = 16
D = 256
H = 16
HD = 16
T = 2048
TC = 1601
CH = 512
QTERM = (0, 0, 0, 1, 1, 2)
KTERM = (0, 1, 2, 0, 1, 0)
TW = 2120
NKT = 17
KR = 100
MR = 97
NEG = -4.0e9
VW = 288
LEAD = 7
DL = (5, 7, 4, 4, 2, 3)


class Eng:

    def __init__(self, name, sem):
        self.name, self.sem, self.n, self.q, self.seen = name, sem, 0, [], {}

    def wait(self, *toks):
        for t in toks:
            if t is None:
                continue
            if isinstance(t, list):
                self.wait(*t)
                continue
            s, v = t
            if self.seen.get(s.name, 0) < v:
                self.seen[s.name] = v
                self.q.append(("w", s, v))

    def op(self, fn, *after, sig=True):
        self.wait(*after)
        if sig:
            self.n += 1
            self.q.append(("i", fn, self.sem, 1))
            return (self.sem, self.n)
        self.q.append(("i", fn, None, 0))
        return None

    def emit(self, eng, q=None):
        for it in self.q if q is None else q:
            if it[0] == "w":
                eng.wait_ge(it[1], it[2])
            elif it[0] == "b":
                r = eng.value_load(it[1], min_val=0, max_val=1)
                with eng.If(r > 0):
                    self.emit(eng, it[2])
                with eng.Else():
                    self.emit(eng, it[3])
            else:
                r = it[1](eng)
                if it[2] is not None:
                    r.then_inc(it[2], it[3])


class Dma:

    def __init__(self, eng, sems):
        self.eng, self.sems, self.cnt, self.k = eng, sems, [0] * len(sems), 0

    def go(self, pairs, *after):
        k = self.k
        self.k = (k + 1) % len(self.sems)
        s = self.sems[k]
        self.eng.wait(*after)
        if self.cnt[k]:
            self.eng.wait((s, self.cnt[k]))
        for o, i in pairs:
            self.eng.q.append(("i", (lambda e, o=o, i=i: e.dma_start(o, i, allow_slow_non_contiguous=True)), s, 16))
            self.cnt[k] += 16
        return (s, self.cnt[k])

    def all_landed(self):
        for s, c in zip(self.sems, self.cnt):
            if c:
                self.eng.wait((s, c))


def xattn_kernel(nc, I, out):
    ctx = ExitStack()
    with ctx:
        def sb(name, shape, dt):
            return ctx.enter_context(nc.sbuf_tensor(name, shape, dt))

        def sem(name):
            return ctx.enter_context(nc.semaphore(name))

        def dram(name, shape, dt):
            return nc.dram_tensor(name, shape, dt, kind="Internal").ap()

        pe, act, dve, pool, sp = (Eng(n, sem("s_" + n)) for n in ("pe", "act", "dve", "pool", "sp"))
        q = Dma(sp, [sem(f"d{i}") for i in range(24)])

        ps = ctx.enter_context(nc.psum_tensor("ps", [P, 8, 512], F32))

        KS = sb("KS", [KR, H, TW], BF16)
        QS = sb("QS", [KR, H, 2, CH], BF16)
        Vt = sb("Vt", [P, NKT, VW], F32)
        x = sb("x", [P, NT, D], F32)
        PT = sb("PT", [P, 8, CH], F32)
        Oe = sb("Oe", [P, 1, CH], F32)
        ON = sb("ON", [P, 2, CH], F32)
        OD = sb("OD", [P, 2, CH], F32)
        XT = sb("XT", [P, 2, CH], F32)
        xn = sb("xn", [P, 4, D], F32)
        Qf = xn[:, :, :].rearrange("p (a b) n -> p a (b n)", a=2)
        S3 = sb("S3", [P, 3, 2, CH], BF16)
        wA = sb("wA", [P, 2, 768], F32)
        wP = sb("wP", [P, 2, D], F32)
        big = sb("big", [P, 6144], F32)
        identF = sb("identF", [P, P], F32)
        identB = sb("identB", [P, P], BF16)
        negI = sb("negI", [P, P], BF16)
        vb = sb("vb", [P, D], F32)
        GBt = sb("GBt", [P, 2, 2, D], F32)
        G = sb("G", [P, 3, 2, D], F32)
        colb = sb("colb", [P, 32], F32)
        modT = sb("modT", [P, 18, 2], F32)
        st = sb("st", [P, 4, 6], F32)
        mv = sb("mv", [P, 4, 2], F32)
        rs = sb("rs", [P, 4], F32)
        mh = sb("mh", [P, 4], F32)
        mx = sb("mx", [P, 2, 16, 4], F32)
        nm = sb("nm", [P, 2, 16], F32)
        mr = sb("mr", [16, 2, 3, P], BF16)
        mf = sb("mf", [16, 2, P], F32)
        dd = sb("dd", [P, 2, 64], F32)

        w1 = big[:, 0:2048].rearrange("p (a n) -> p a n", a=2)
        w2 = big[:, 2048:4096].rearrange("p (a n) -> p a n", a=8)
        HT = big[:, 4096:6144].rearrange("p (a n) -> p a n", a=8)
        maskT = big[:, 0:4096].bitcast(BF16).rearrange("p (k n) -> p k n", k=NT)
        mstg = big[:, 4096:4608].bitcast(I32)
        mbf = big[:, 4608:4864].bitcast(BF16)
        keep = big[:, 4864:5120].bitcast(BF16)
        onesB = big[:, 5120:5184].bitcast(BF16)

        scr = [dram(f"scr{i}", [3, D, CH], BF16) for i in range(6)]
        scr_m = dram("scr_m", [4, 3, 4, CH], BF16)
        scr_d = dram("scr_d", [2, H, CH], F32)
        scr_r = dram("scr_r", [2, H, CH], F32)

        tok = {}

        def get(*keys):
            return [tok.get(k) for k in keys]

        def add(key, t):
            tok[key] = tok.get(key, []) + [t]

        m0 = pool.op(lambda e: e.memset(identF[:], 0.0))
        m1 = pool.op(lambda e: e.affine_select(out=identF[:], in_=identF[:], compare_op=ALU.not_equal, fill=1.0,
                                               base=0, pattern=[[-1, P]], channel_multiplier=1), m0)
        m2 = pool.op(lambda e: e.tensor_copy(identB[:], identF[:]), m1)
        m3 = pool.op(lambda e: e.tensor_scalar(negI[:], identF[:], NEG, None, ALU.mult), m1)
        m4 = pool.op(lambda e: e.memset(mh[:], -0.5), m3)
        ident = [m1, m2, m3, m4]
        S3f = S3[:, :, :, :].rearrange("p t a n -> p (t a n)")
        consts = []

        class Ring:
            def __init__(self, n):
                self.n, self.i, self.free = n, 0, [None] * n

            def take(self):
                s = self.i % self.n
                self.i += 1
                return s, self.free[s]

        M, A = Ring(2), Ring(3)

        def mslot(s):
            return ps[:, 3 + 2 * s:5 + 2 * s, :]

        def mflat(s):
            return mslot(s).rearrange("p a n -> p (a n)")

        def load_x(c, *after):
            tok["x", c] = [q.go([(x[:, 4 * c:4 * c + 4, :],
                                  I["x"][0, 512 * c:512 * c + 512, :].rearrange("(t p) d -> p t d", p=P))], *after)]


        def load_cols(dst, vec):
            return (dst, vec.rearrange("(c p) -> p c", p=P))

        def load_w(dst, w):
            return (dst, w.rearrange("(a p) n -> p a n", p=P))

        adw = [w.rearrange("p (a n) -> p a n", a=2) for w in (
            PT[:, 0:3, :].rearrange("p a n -> p (a n)"), big[:, 0:1536], big[:, 2048:3584])]
        cT = sb("cT", [P, 2, 2], F32)
        ce = sb("ce", [P, 2, 2], F32)
        adb = sb("adb", [P, 18], F32)
        cb = Oe[:, 0, :].rearrange("p (a r n) -> p a r n", a=2, r=2)
        bb = ON[:, :, :].rearrange("p a n -> p (a n)")

        def load_ada(g):
            return q.go([(adw[g], I["L0_xattn_ada_w"][:, 768 * g:768 * g + 768].rearrange("(a p) n -> p a n", p=P))])

        t_c = q.go([(cT[:, a, r:r + 1], I["ctx_1024"][0, r, 128 * a:128 * a + 128].rearrange("(p o) -> p o", o=1))
                    for a in range(2) for r in range(2)])
        load_x(0)
        t_ada = [load_ada(0)]
        t_adb = q.go([load_cols(adb[:], I["L0_xattn_ada_b"])])
        tok["wA"] = [q.go([load_w(wA[:], I["L0_xattn_attn_qkv_w"])])]
        load_x(1)
        tok["colb"] = [q.go([load_cols(colb[:, o:o + v.shape[0] // P], v) for o, v in (
            (0, I["L0_xattn_attn_qkv_b"][0:512]), (4, I["L0_xattn_crs_qkv_b"][0:512]),
            (8, I["L1_xattn_sa_qb"]), (10, I["L1_xattn_sa_kb"]), (12, I["L1_xattn_ca_qb"]), (14, I["L1_xattn_ca_kb"]),
            (16, I["L0_xattn_mlp_fc1_b"]), (24, I["L1_xattn_b1"]))])]
        tok["vb"] = [q.go([(vb[:], I["L0_xattn_attn_qkv_b"][512:768].partition_broadcast(P))])]
        t_bb = q.go([(bb[:, 256 * g:256 * g + 256],
                      I["L0_xattn_ada_b"][768 * g + 512:768 * g + 768].partition_broadcast(P)) for g in range(3)])
        o1 = dve.op(lambda e: e.memset(S3f[0:1, 0:TW].bitcast(I32), 0x3F803F80))
        o2 = dve.op(lambda e: e.memset(S3f[32:33, 0:TW].bitcast(I32), 0))
        tok["s3_rd"] = [q.go(
            [(KS[r:r + 1, :, :], S3f[0:1, 0:TW].rearrange("a (k n) -> a k n", k=1).to_broadcast([1, H, TW]))
             for r in (97, 98, 99)]
            + [(KS[96:97, :, :], S3f[32:33, 0:TW].rearrange("a (k n) -> a k n", k=1).to_broadcast([1, H, TW]))]
            + [(QS[96:97, :, :, :].rearrange("a h s n -> a h (s n)"),
                S3f[0:1, 0:2 * CH].rearrange("a (k n) -> a k n", k=1).to_broadcast([1, H, 2 * CH]))], o1, o2)]
        load_x(2)
        load_x(3)
        t_ada += [load_ada(1), load_ada(2)]

        e1 = act.op(lambda e: e.activation(ce[:], cT[:], ACT.Exp, scale=-1.0), t_c)
        e2 = dve.op(lambda e: e.tensor_scalar(ce[:], ce[:], 1.0, None, ALU.add), e1)
        e3 = dve.op(lambda e: e.reciprocal(ce[:], ce[:]), e2)
        e4 = dve.op(lambda e: e.tensor_tensor(cT[:], cT[:], ce[:], ALU.mult), e3)
        e5 = dve.op(lambda e: e.tensor_copy(cb, cT[:].rearrange("p a (r o) -> p a r o", o=1)
                                            .to_broadcast([P, 2, 2, P])), e4)
        tok["oe_rd", 0] = []

        def modulation(g):
            s, fr = M.take()
            mf_ = mflat(s)
            dst = adw[g]
            for j in range(6):
                for a in range(2):
                    t1 = pe.op(lambda e, j=j, a=a: e.matmul(
                        mf_[:, 2 * j:2 * j + 2], dst[:, a, 128 * j:128 * j + 128], cT[:, a, :],
                        start=a == 0, stop=a == 1), t_ada[g], e4, fr, sig=(j == 5 and a == 1))
            for r in range(2):
                for a in range(2):
                    t2 = pe.op(lambda e, r=r, a=a: e.matmul(
                        mf_[:, 512 + 256 * r:768 + 256 * r], cb[:, a, r, :], dst[:, a, 512:768],
                        start=a == 0, stop=a == 1), e5, sig=(r == 1 and a == 1))
            tok[("pt_rd", 0) if g == 0 else ("ms_rd", g - 1)] = [t2]
            tok["oe_rd", 0] = [t2]
            u1 = dve.op(lambda e: e.tensor_tensor(
                modT[:, 6 * g:6 * g + 6, :], mf_[:, 0:12].rearrange("p (j r) -> p j r", r=2),
                adb[:, 6 * g:6 * g + 6].rearrange("p (j o) -> p j o", o=1).to_broadcast([P, 6, 2]), ALU.add), t1, t_adb)
            u2 = dve.op(lambda e: e.tensor_scalar(modT[:, 6 * g + 2:6 * g + 4, :], modT[:, 6 * g + 2:6 * g + 4, :],
                                                  1.0, None, ALU.add), u1)
            for r in range(2):
                u3 = dve.op(lambda e, r=r: e.tensor_tensor(
                    G[:, g, r, :], mf_[:, 512 + 256 * r:768 + 256 * r], bb[:, 256 * g:256 * g + 256], ALU.add),
                    t2, t_bb)
            M.free[s] = u3
            tok["mod", g] = [u2, u3]
            tok["bb_free"] = [u3]

        def ln_stats(c, eps):
            for t in range(4):
                a = dve.op(lambda e, t=t: e.bn_stats(st[:, t, :], x[:, 4 * c + t, :]), get(("x", c)), sig=t == 3)
            for t in range(4):
                b = dve.op(lambda e, t=t: e.bn_aggr(mv[:, t, :], st[:, t, :]), a, get("mv_rd"), sig=t == 3)
            d = pool.op(lambda e: e.tensor_scalar(rs[:], mv[:, :, 1], eps, None, ALU.add), b, get("rs_rd"))
            f = pool.op(lambda e: e.tensor_tensor(rs[:], rs[:], mh[:], ALU.pow), d)
            tok["rs"] = [f]
            tok["mv_rd"] = [d]

        def ln_xn(c):
            for t in range(4):
                a = dve.op(lambda e, t=t: e.tensor_scalar(xn[:, t, :], x[:, 4 * c + t, :], mv[:, t, 0:1],
                                                          rs[:, t:t + 1], ALU.subtract, ALU.mult),
                           get("rs", "xn_rd"), sig=t == 3)
            tok["xn"] = [a]
            tok["rs_rd"] = [a]
            add(("x_rd", c), a)

        at = {"xt": XT, "qf": Qf, "quick": False, "tail": False}

        def transpose_in(src, n, wr, scale=None, shift=None):
            s, fr = M.take()
            XT = at["xt"]
            for a in range(2):
                for t in range((n + 127) // 128):
                    w = min(128, n - 128 * t)
                    z = pe.op(lambda e, t=t, a=a, w=w: e.transpose(
                        mslot(s)[:, a, 128 * t:128 * t + w], src[0:w, t, 128 * a:128 * a + 128], identF[0:w, 0:w]),
                        wr, fr, ident)
            for a in range(2):
                if scale is None:
                    if a == 0:
                        v0 = act.op(lambda e: e.copy(XT[:, 0, 0:n], mslot(s)[:, 0, 0:n]), z, get("xt_rd"))
                    else:
                        v1 = dve.op(lambda e: e.tensor_copy(XT[:, 1, 0:n], mslot(s)[:, 1, 0:n]), z, get("xt_rd"))
                elif a == 0:
                    v0 = act.op(lambda e: e.activation(XT[:, 0, 0:n], mslot(s)[:, 0, 0:n], ACT.Identity,
                                                       bias=shift[0], scale=scale[0]), z, get("xt_rd"))
                else:
                    v1 = act.op(lambda e: e.activation(XT[:, 1, 0:n], mslot(s)[:, 1, 0:n], ACT.Identity,
                                                       bias=shift[1], scale=scale[1]), z, get("xt_rd"))
            M.free[s] = [v0, v1]
            tok["xt"] = [v0, v1]
            return z

        def mod_xt(c, g):
            r = c // 2
            z = transpose_in(xn, 512, get("xn", ("mod", g)),
                             [modT[:, 6 * g + 2 + a, r:r + 1] for a in range(2)],
                             [modT[:, 6 * g + a, r:r + 1] for a in range(2)])
            tok["xn_rd"] = [z]

        nscr = [0]

        def proj_split(n, woff, bcol, dst, wr, terms):
            s, fr = M.take()
            XT, Qf, quick = at["xt"], at["qf"], at["quick"]
            rd_ = "qf_rd" if quick else "xn_rd"
            for oc in range(2):
                for a in range(2):
                    z = pe.op(lambda e, oc=oc, a=a: e.matmul(
                        mslot(s)[:, oc, 0:n], wA[:, a, woff + 128 * oc:woff + 128 * oc + 128], XT[:, a, 0:n],
                        start=a == 0, stop=a == 1), fr, get("xt", "wA"), sig=(oc == 1 and a == 1))
            tok["xt_rd"] = [z]
            tok["wA_rd"] = [z]
            f0 = act.op(lambda e: e.activation(Qf[:, 0, 0:n], mslot(s)[:, 0, 0:n], ACT.Identity,
                                               bias=colb[:, bcol:bcol + 1]), z, get(rd_, "colb"))
            f1 = dve.op(lambda e: e.tensor_scalar(Qf[:, 1, 0:n], mslot(s)[:, 1, 0:n], colb[:, bcol + 1:bcol + 2],
                                                  None, ALU.add), z, get(rd_, "colb"))
            f = [f0, f1]
            M.free[s] = f
            h = act.op(lambda e: e.copy(S3[:, 0, :, 0:n], Qf[:, :, 0:n]), f, get("s3_rd"))
            by = dve if quick else pool
            r1 = by.op(lambda e: e.tensor_tensor(Qf[:, :, 0:n], Qf[:, :, 0:n], S3[:, 0, :, 0:n], ALU.subtract), f, h)
            m = dve.op(lambda e: e.tensor_copy(S3[:, 1, :, 0:n], Qf[:, :, 0:n]), r1)
            l = by.op(lambda e: e.tensor_tensor(S3[:, 2, :, 0:n], Qf[:, :, 0:n], S3[:, 1, :, 0:n], ALU.subtract), m)
            tok[rd_] = [l]
            k = nscr[0] % len(scr)
            nscr[0] += 1
            w = q.go([(scr[k][:, 128 * oc:128 * oc + 128, 0:n].rearrange("t p n -> p t n"), S3[:, :, oc, 0:n])
                      for oc in range(2)], h, m, l, get(("scr_rd", k)))
            tok["s3_rd"] = [w]
            rd = q.go([(dst(16 * r), scr[k][t, :, 0:n].rearrange("(h d) n -> d h n", d=HD))
                       for r, t in enumerate(terms)], w, wr)
            tok["scr_rd", k] = [rd]
            return rd

        def proj_q(c, slot, bc):
            tok["qs", slot] = [proj_split(512, 0, bc, lambda lo: QS[lo:lo + 16, :, slot, :],
                                          get(("qs_rd", slot)), QTERM)]

        def proj_k(col, n, key, rd, bc):
            tok[key] = [proj_split(n, 256, bc + 2, lambda lo: KS[lo:lo + 16, :, col:col + n], rd, KTERM)]

        def proj_v(kt0, n, key, rd, woff=512):
            s, fr = M.take()
            XT = at["xt"]
            nt = (n + 127) // 128
            w = min(n, 128)
            for t in range(nt):
                for a in range(2):
                    z = pe.op(lambda e, t=t, a=a: e.matmul(
                        mflat(s)[0:w, 256 * t:256 * t + 256], XT[:, a, 128 * t:128 * t + w], wA[:, a, woff:woff + 256],
                        start=a == 0, stop=a == 1), fr, get("xt", "wA"), sig=(t == nt - 1 and a == 1))
            tok["xt_rd"] = [z]
            tok["wA_rd"] = [z]
            vv = Vt[0:w, kt0:kt0 + nt, 0:272].rearrange("p t (h d) -> p t h d", d=17)
            for t in range(nt):
                v = dve.op(lambda e, t=t: e.tensor_tensor(
                    vv[:, t, :, 0:16], mflat(s)[0:w, 256 * t:256 * t + 256].rearrange("p (h d) -> p h d", d=16),
                    vb[0:w, :].rearrange("p (h d) -> p h d", d=16), ALU.add), z, rd, get("vb"), consts, sig=t == nt - 1)
            M.free[s] = v
            tok["vb_rd"] = [v]
            tok[key] = [v]

        um = [0]
        nm4 = [0]
        uo = [0]

        def max_tasks(hg, qs, keys, masked, kdep, early=None):
            b = um[0] % 2
            um[0] += 1
            parts = [(lo, min(keys[1], lo + 512)) for lo in range(keys[0], keys[1], 512)]
            tasks = []
            last = {}

            def quantum(pp, tq, i, lo, hi):
                s, fr = M.take()
                pr, n = 2 * hg + pp, hi - lo
                for u in range(2):
                    z = pe.op(lambda e, u=u: e.matmul(
                        mslot(s)[:, u, 0:n], QS[0:MR, 2 * pr + u, qs, 128 * tq:128 * tq + 128],
                        KS[0:MR, 2 * pr + u, lo:hi], start=True, stop=not masked),
                        fr, get(("qs", qs)), kdep if early is None else get(("k", i)), consts, sig=u == 1)
                for u in range(2 if masked else 0):
                    for kk in range(n // 128):
                        z = pe.op(lambda e, u=u, kk=kk: e.matmul(
                            mslot(s)[:, u, 128 * kk:128 * kk + 128],
                            maskT[:, lo // 128 + kk, 128 * tq:128 * tq + 128], negI[:],
                            start=False, stop=kk == n // 128 - 1), get("maskT"), ident,
                            sig=(u == 1 and kk == n // 128 - 1))
                o = mx[:, b, :, i].rearrange("p (h k) -> p h k", k=4)[:, 2 * pp:2 * pp + 2, tq:tq + 1]
                M.free[s] = dve.op(lambda e: e.tensor_reduce(
                    out=o, in_=mslot(s)[:, :, 0:n], axis=AX.X, op=ALU.max), z, get(("mx_rd", b)))
                last["r"] = M.free[s]
                last["z"] = z

            def narrow(pp, i, lo, hi):
                s, fr = M.take()
                pr, n = 2 * hg + pp, hi - lo
                for u in range(2):
                    for tq in range(4):
                        z = pe.op(lambda e, u=u, tq=tq: e.matmul(
                            mslot(s)[:, u, n * tq:n * tq + n], QS[0:MR, 2 * pr + u, qs, 128 * tq:128 * tq + 128],
                            KS[0:MR, 2 * pr + u, lo:hi], start=True, stop=True),
                            fr, get(("qs", qs)), kdep, consts, sig=(u == 1 and tq == 3))
                M.free[s] = dve.op(lambda e: e.tensor_reduce(
                    out=mx[:, b, :, i].rearrange("p (h k) -> p h k", k=4)[:, 2 * pp:2 * pp + 2, :],
                    in_=mslot(s)[:, :, 0:4 * n].rearrange("p u (k n) -> p u k n", n=n), axis=AX.X, op=ALU.max),
                    z, get(("mx_rd", b)))
                last["r"] = M.free[s]
                last["z"] = z

            if early is not None:
                for i, (lo, hi) in enumerate(parts):
                    tasks.extend(early[i:i + 1])
                    tasks.extend(lambda a=(pp, tq, i, lo, hi): quantum(*a) for pp in range(2) for tq in range(4))
            for pp in range(2) if early is None else ():
                for i, (lo, hi) in enumerate(parts):
                    if hi - lo < 128:
                        tasks.append(lambda a=(pp, i, lo, hi): narrow(*a))
                for tq in range(4):
                    for i, (lo, hi) in enumerate(parts):
                        if hi - lo >= 128:
                            tasks.append(lambda a=(pp, tq, i, lo, hi): quantum(*a))

            def fin_a():
                np_ = len(parts)
                last["a"] = a = dve.op(lambda e: e.tensor_reduce(out=nm[:, b, :], in_=mx[:, b, :, 0:np_], axis=AX.X, op=ALU.max,
                                                     negate=True), last["r"], get(("nm_rd", b)))
                tok["mx_rd", b] = [a]

            def fin_b():
                a = last["a"]
                s, fr = M.take()
                z = pe.op(lambda e: e.transpose(mflat(s)[0:16, 0:128], nm[:, b, :], identF[:]), a, fr, ident)
                tok["nm_rd", b] = [z]
                src = mflat(s)[0:16, 0:128]
                h1 = dve.op(lambda e: e.tensor_copy(mr[:, b, 0, :], src), z, get(("mr_rd", b)))
                f1 = dve.op(lambda e: e.tensor_tensor(mf[:, b, :], src, mr[:, b, 0, :], ALU.subtract), h1)
                M.free[s] = f1
                h2 = dve.op(lambda e: e.tensor_copy(mr[:, b, 1, :], mf[:, b, :]), f1)
                h3 = dve.op(lambda e: e.tensor_tensor(mr[:, b, 2, :], mf[:, b, :], mr[:, b, 1, :], ALU.subtract), h2)
                d4 = nm4[0] % 4
                nm4[0] += 1
                w = q.go([(scr_m[d4].rearrange("t h (k c) -> (h k) t c", c=128), mr[:, b, :, :])],
                         h1, h2, h3, get(("scrm_rd", d4)))
                tok["mr_rd", b] = [w]
                rd = q.go([(QS[97:100, 4 * hg:4 * hg + 4, qs, :], scr_m[d4])], w, last["z"], get(("qs_rd", qs)))
                tok["scrm_rd", d4] = [rd]
                tok["m", hg, qs] = [rd]
            return tasks + [fin_a, fin_b]

        def exp_steps(hg, qs, ob, kts, masked, kdep, vdep):
            steps = []
            state = {}

            def s_step(i, pp):
                col, vt, n = kts[i]
                pr = 2 * hg + pp
                (a0, f0), (a1, f1) = A.take(), A.take()
                bk = (a0, a1)
                for u in range(2):
                    state["s", u] = z = pe.op(lambda e, u=u: e.matmul(
                        ps[0:n, bk[u], :], KS[0:KR, 2 * pr + u, col:col + n], QS[0:KR, 2 * pr + u, qs, :],
                        start=True, stop=not masked),
                        (f0, f1)[u], get(("qs", qs), ("m", hg, qs)), kdep, consts)
                for u in range(2 if masked else 0):
                    z = pe.op(lambda e, u=u: e.matmul(ps[0:n, bk[u], :], negI[:], maskT[:, vt, :],
                                                      start=False, stop=True), get("maskT"), ident)
                    state["s", u] = z
                for u in range(2):
                    x_ = act.op(lambda e, u=u: e.activation(PT[0:n, (i % 2) * 4 + 2 * pp + u, :], ps[0:n, bk[u], :],
                                                            ACT.Exp, scale=0.25),
                                state["s", u], get(("pt_rd", i % 2)))
                    A.free[bk[u]] = x_
                    state["x", i, 2 * pp + u] = x_
                state["z"] = z

            def pv(i):
                col, vt, n = kts[i]
                for j in range(4):
                    z = pe.op(lambda e, j=j: e.matmul(
                        ps[32 * j:32 * j + 32, 7, :], Vt[0:n, vt, 17 * (4 * hg + j):17 * (4 * hg + j) + 32],
                        PT[0:n, (i % 2) * 4 + j, :],
                        start=i == 0, stop=i == len(kts) - 1, tile_position=(0, 32 * j)),
                        [state["x", i, j]], get("o_free"), vdep, sig=j == 3)
                tok["pt_rd", i % 2] = [z]
                state["pv"] = z

            for i in range(len(kts)):
                for pp in range(2):
                    def f(i=i, pp=pp):
                        s_step(i, pp)
                        if pp == 1 and i > 0:
                            pv(i - 1)
                    steps.append(f)

            def end():
                pv(len(kts) - 1)
                b = 0
                uo[0] += 1
                e_ = act.op(lambda e: e.copy(Oe[:, b, :], ps[:, 7, :]), state["pv"], get(("oe_rd", b)))
                tok["o_free"] = [e_]
                tok["qs_rd", qs] = [state["z"]]
                w1_ = q.go([(ON[64 * (hg % 2) + 16 * j:64 * (hg % 2) + 16 * j + 16, hg // 2, :],
                             Oe[32 * j:32 * j + 16, b, :]) for j in range(4)]
                           + [(scr_d[ob, 4 * hg:4 * hg + 4, :], Oe[16:128:32, b, :])],
                           e_, get("on_rd", ("scrd_rd", ob), "bb_free"))
                tok["oe_rd", b] = [w1_]
                add("on", w1_)
            steps.append(end)
            return steps

        def norm(ob):
            hold = {}

            def na():
                hold["r"] = q.go([(dd[:, ob, :], scr_d[ob].rearrange("h (s c) -> (h s) c", c=64))],
                                 get("on", ("dd_rd", ob)))
                tok["scrd_rd", ob] = [hold["r"]]

            def nb():
                a = dve.op(lambda e: e.reciprocal(dd[:, ob, :], dd[:, ob, :]), hold["r"])
                w = q.go([(scr_r[ob].rearrange("h (s c) -> (h s) c", c=64), dd[:, ob, :])], a, get(("scrr_rd", ob)))
                tok["dd_rd", ob] = [w]
                hold["g"] = q.go([(OD[:, k, :], bass.AP(scr_r.tensor, scr_r[ob, 8 * k, 0:1].offset,
                                                        [[CH, 8], [0, 16], [1, CH]])) for k in range(2)],
                                 w, get("od_rd"))
                tok["scrr_rd", ob] = [hold["g"]]

            def nc_():
                m = (dve if at["tail"] else pool).op(lambda e: e.tensor_tensor(OD[:], ON[:], OD[:], ALU.mult),
                                                     hold["g"], get("on"))
                tok["ot"] = [m]
                tok["on_rd"] = [m]
                tok["on"] = []
            def done():
                pass
            norms.extend([(0, na), (DL[0], nb), (DL[1], nc_), (DL[2], done)])

        def residual_l0(c, s, z, g, lo=0, nt=4):
            r, gbi = c // 2, g % 2
            t1 = dve.op(lambda e: e.tensor_tensor(
                xn[:, lo:lo + nt, :], mflat(s)[:, 0:256 * nt].rearrange("p (t n) -> p t n", n=256),
                G[:, g, r:r + 1, :].to_broadcast([P, nt, D]), ALU.mult), z, get("xn_rd", ("mod", g)))
            M.free[s] = t1
            xs = x[:, 4 * c + lo:4 * c + lo + nt, :]
            t2 = pool.op(lambda e: e.tensor_tensor(xs, xs, xn[:, lo:lo + nt, :], ALU.add), t1, get(("x", c), ("x_rd", c)))
            t3 = pool.op(lambda e: e.tensor_tensor(xs, xs, GBt[:, gbi, r:r + 1, :].to_broadcast([P, nt, D]), ALU.add),
                         t2, get(("gb", gbi)))
            tok["gb_rd", gbi] = [t3]
            tok["xn_rd"] = [t2]
            add(("x", c), t3)

        def residual_l1(c, s, z, gbi, lo=0, nt=4):
            xs = x[:, 4 * c + lo:4 * c + lo + nt, :]
            t1 = dve.op(lambda e: e.tensor_tensor(
                xs, mflat(s)[:, 0:256 * nt].rearrange("p (t n) -> p t n", n=256), xs, ALU.add),
                z, get(("x", c), ("x_rd", c)))
            M.free[s] = t1
            i, r = gbi
            t3 = (dve if at["tail"] else pool).op(lambda e: e.tensor_tensor(xs, xs, GBt[:, i, r:r + 1, :].to_broadcast([P, nt, D]), ALU.add),
                         t1, get(("gb", gbi)))
            tok["gb_rd", i] = [t3]
            add(("x", c), t3)

        def outproj(c, res):
            s, fr = M.take()
            for t in range(4):
                for a in range(2):
                    z = pe.op(lambda e, t=t, a=a: e.matmul(
                        mflat(s)[:, 256 * t:256 * t + 256], OD[:, a, 128 * t:128 * t + 128], wP[:, a, :],
                        start=a == 0, stop=a == 1), fr, get("ot", "wP"), sig=(t == 3 and a == 1))
            tok["od_rd"] = [z]
            tok["wP_rd"] = [z]
            res(c, s, z)

        def ln_l1(c, gl):
            def scale():
                for t in range(4):
                    xs = x[:, 4 * c + t, :]
                    a = dve.op(lambda e, t=t, xs=xs: e.tensor_scalar(
                        xs, xs, mv[:, t, 0:1], rs[:, t:t + 1], ALU.subtract, ALU.mult), get("rs", ("x", c)), sig=t == 3)
                tok["rs_rd"] = [a]
                xs = x[:, 4 * c:4 * c + 4, :]
                by = dve if at["tail"] else pool
                b = by.op(lambda e: e.tensor_tensor(xs, xs, G[:, gl, 0:1, :].to_broadcast([P, 4, D]), ALU.mult),
                          a, get(("lnp", gl)))
                d = by.op(lambda e: e.tensor_tensor(xs, xs, G[:, gl, 1:2, :].to_broadcast([P, 4, D]), ALU.add), b)
                tok["x", c] = [d]
            return [(DL[3], lambda: ln_stats(c, 1e-5)), (DL[4], scale)]

        def mlp_hid(c, fn, bc, hf, hp):
            s, fr = M.take()
            for i in range(4):
                for a in range(2):
                    z = pe.op(lambda e, i=i, a=a: e.matmul(
                        mflat(s)[:, 256 * i:256 * i + 256],
                        w1[:, a, 128 * (4 * hp + i):128 * (4 * hp + i) + 128],
                        XT[:, a, 256 * hf:256 * hf + 256], start=a == 0, stop=a == 1),
                        fr, get("xt", "w1"), sig=(i == 3 and a == 1))
            tok["xt_rd"] = [z]
            if fn == ACT.Relu:
                vs = []
                for i in range(4):
                    hc = 4 * hp + i
                    if i < 2:
                        vs.append(act.op(lambda e, i=i, hc=hc: e.activation(
                            HT[:, hc, :], mflat(s)[:, 256 * i:256 * i + 256], fn, bias=colb[:, bc + hc:bc + hc + 1]),
                            z, get("ht_rd", "colb")))
                    else:
                        vs.append(dve.op(lambda e, i=i, hc=hc: e.tensor_scalar(
                            HT[:, hc, :], mflat(s)[:, 256 * i:256 * i + 256], colb[:, bc + hc:bc + hc + 1], 0.0,
                            ALU.add, ALU.max), z, get("ht_rd", "colb")))
                M.free[s] = vs
                tok["ht", hp] = vs
                return
            for i in range(4):
                v = act.op(lambda e, i=i, hc=4 * hp + i: e.activation(
                    HT[:, hc, :], mflat(s)[:, 256 * i:256 * i + 256], fn, bias=colb[:, bc + hc:bc + hc + 1]),
                    z, get("ht_rd", "colb"), sig=i == 3)
            M.free[s] = v
            tok["colb_rd"] = [v]
            tok["ht", hp] = [v]

        def mlp_out(c, hf, res):
            s, fr = M.take()
            for t in range(2):
                for hc in range(8):
                    z = pe.op(lambda e, t=t, hc=hc: e.matmul(
                        mflat(s)[:, 256 * t:256 * t + 256], HT[:, hc, 128 * t:128 * t + 128], w2[:, hc, :],
                        start=hc == 0, stop=hc == 7), fr, get(("ht", 0), ("ht", 1), "w2"),
                        sig=(t == 1 and hc == 7))
            tok["ht_rd"] = [z]
            tok["w_rd"] = [z]
            res(c, s, z, lo=2 * hf, nt=2)

        def mlp_chain(c, fn, bc, res):
            return [(2, lambda: mlp_hid(c, fn, bc, 0, 0)), (0, lambda: mlp_hid(c, fn, bc, 0, 1)),
                    (2, lambda: mlp_out(c, 0, res)),
                    (1, lambda: mlp_hid(c, fn, bc, 1, 0)), (0, lambda: mlp_hid(c, fn, bc, 1, 1)),
                    (2, lambda: mlp_out(c, 1, res))]

        urgent, lazy, cur, since, side, norms, nsince = [], [], [], [0], [], [], [0]

        def flush_norms(keep=0):
            while len(norms) > keep:
                norms.pop(0)[1]()
            nsince[0] = 0

        def bg_step(force=False):
            since[0] += 1
            if norms:
                nsince[0] += 1
                if norms[0][0] <= nsince[0]:
                    norms.pop(0)[1]()
                    nsince[0] = 0
            while True:
                if not cur:
                    if urgent:
                        cur.extend(urgent.pop(0)[1])
                    elif lazy:
                        cur.extend(lazy.pop(min(range(len(lazy)), key=lambda i: (lazy[i][0], i)))[1])
                    else:
                        return
                wait = cur[0][0]
                if force:
                    if wait is None:
                        flush_norms()
                elif (norms if wait is None else wait > since[0]):
                    return
                _, f = cur.pop(0)
                f()
                since[0] = 0
                if not (cur and cur[0][0] == 0):
                    return

        def bg_until(k):
            while urgent or any(d <= k for d, _ in lazy) or (cur and k >= 0):
                bg_step(True)

        def drain(chain):
            flush_norms()
            for _, f in chain:
                f()

        def attention(seq, first=True, beyond=None, beside=(), early=None):
            def start(n, early=None):
                ph, c, qs, hg = seq[n] if n < len(seq) else beyond
                return max_tasks(hg, qs, ph.keys(c), ph.masked, ph.kdep(c), early)

            total = len(seq) + (beyond is not None)
            if first:
                for j, f in enumerate(start(0, early)):
                    f()
                    if j % 3 == 1 and j // 3 < len(beside):
                        beside[j // 3]()
            size = [2 * len(ph.kts(c)) for ph, c, _, _ in seq]
            begin = [sum(size[:i]) for i in range(len(seq))]
            opens = [0] + [max(begin[k - 1] + 1, begin[k - 1] + size[k - 1] - LEAD) for k in range(1, total)]
            k, left, m, step = 0, [], 0, 0
            for i, (ph, c, qs, hg) in enumerate(seq):
                fg = exp_steps(hg, qs, c % 2, ph.kts(c), ph.masked, ph.kdep(c), ph.vdep(c))
                for f in fg[:-1]:
                    f()
                    if not left and k + 1 < total and (k == 0 or step >= opens[k]):
                        k += 1
                        if (seq[k] if k < len(seq) else beyond)[3] == 0:
                            bg_until(unit0[0] + k)
                        left = start(k)
                        m = len(left)
                        lo = step
                        span = max(1, opens[k] - lo)
                    step += 1
                    if left:
                        want = m if step - lo >= span else -(-(step - lo) * m // span)
                        while m - len(left) < min(want, m):
                            left.pop(0)()
                    if side and step % 4 == 3:
                        side.pop(0)()
                    bg_step()
                if k == i + 1:
                    while left:
                        left.pop(0)()
                if hg == 0:
                    flush_norms(1)
                fg[-1]()
                if hg == 3:
                    u, l = ph.post(c, qs)
                    urgent.extend(u)
                    lazy.extend(l)
            unit0[0] += len(seq)

        unit0 = [0]

        def load_wA(wlist, vbias):
            tok["wA"] = [q.go([load_w(wA[:, :, o:o + w.shape[1]], w) for o, w in wlist], get("wA_rd"))]
            tok["vb"] = [q.go([(vb[:], vbias.partition_broadcast(P))], get("vb_rd"))]

        def load_wP(w):
            tok["wP"] = [q.go([load_w(wP[:], w)], get("wP_rd"))]

        def load_mlp(a, b, *after):
            tok["w1"] = [q.go([load_w(w1, a)], get("w_rd"), *after)]
            tok["w2"] = [q.go([load_w(w2, b)], get("w_rd"), *after)]

        def gate_bias(g, b):
            gbi = g % 2
            a = q.go([(GBt[:, gbi, r, :], b.partition_broadcast(P)) for r in range(2)], get(("gb_rd", gbi)))
            d = pool.op(lambda e: e.tensor_tensor(GBt[:, gbi], GBt[:, gbi], G[:, g, :, :], ALU.mult),
                        a, get(("mod", g)))
            tok["gb", gbi] = [d]

        def plain_bias(gbi, b):
            tok["gb", gbi] = [q.go([(GBt[:, gbi[0], gbi[1], :], b.partition_broadcast(P))], get(("gb_rd", gbi[0])))]

        def load_lnp(i, *after):
            tok["lnp", i] = [q.go([(G[:, i, j, :], I[f"L1_xattn_{n}{i + 1}"].partition_broadcast(P))
                                   for j, n in enumerate(("g", "be"))], *after)]

        def l0_weights(nm_):
            load_wA([(0, I[f"L0_xattn_{nm_}_qkv_w"])], I[f"L0_xattn_{nm_}_qkv_b"][512:768])

        def need_q(p):
            if tok.get("have_q") != p:
                tok["have_q"] = p
                tok["wA"] = tok["wA"] + [q.go([load_w(wA[:, :, 0:256], I[f"L1_xattn_{p}_qw"])], get("wA_rd"))]

        def need_kv(p):
            if tok.get("have_kv") != p:
                tok["have_kv"] = p
                tok["wA"] = tok["wA"] + [q.go([load_w(wA[:, :, 256:512], I[f"L1_xattn_{p}_kw"]),
                                               load_w(wA[:, :, 512:768], I[f"L1_xattn_{p}_vw"])], get("wA_rd"))]
                tok["vb"] = [q.go([(vb[:], I[f"L1_xattn_{p}_vb"].partition_broadcast(P))], get("vb_rd"))]

        def need_o(p):
            if tok.get("have_o") != p:
                tok["have_o"] = p
                load_wP(I[f"L1_xattn_{p}_ow"])

        def ln_mod(c, g):
            return [(DL[3], lambda: ln_stats(c, 1e-6)), (DL[4], lambda: ln_xn(c)), (DL[5], lambda: mod_xt(c, g))]

        def kv_l0(c, g, slot=None):
            kr = get("ks_rd", ("half_rd", c // 2))
            return (ln_mod(c, g) + [(1, lambda: proj_k(512 * c, 512, ("k", c), kr, 4 * g)),
                                    (1, lambda: proj_v(4 * c, 512, ("v", c), kr))]
                    + ([(1, lambda: proj_q(c, slot, 4 * g))] if slot is not None else []))

        def q_l0(c, slot, g):
            return ln_mod(c, g) + [(1, lambda: proj_q(c, slot, 4 * g))]

        def x_to_xt(c):
            z = transpose_in(x[:, 4 * c:4 * c + 4, :], 512, get(("x", c)))
            tok["x_rd", c] = [z]

        def x_q(c, slot, p):
            return [(0, lambda: need_q(p)), (4, lambda: x_to_xt(c)),
                    (1, lambda: proj_q(c, slot, 8 if p == "sa" else 12))]

        def out_l0(c, g):
            norm(c % 2)
            ch = [(None, lambda: outproj(c, lambda c, s, z: residual_l0(c, s, z, g)))]
            if g == 1:
                ch = [(0, lambda: load_x(c, get(("x", c), ("x_rd", c))))] + ch
            return ch

        def out_l1(c, p):
            k = 0 if p == "sa" else 1
            norm(c % 2)
            return [(0, lambda: need_o(p)),
                    (None, lambda: outproj(c, lambda c, s, z: residual_l1(c, s, z, (1, k))))] + ln_l1(c, k)

        class Phase:
            def __init__(self, keys, kdep, kts, vdep, post, masked=False):
                self.keys, self.kdep, self.kts, self.vdep, self.post, self.masked = keys, kdep, kts, vdep, post, masked

        def phase_l0(g, post):
            def h(c):
                return (c // 2) ^ g
            return Phase(lambda c: (1024 * h(c), 1024 * h(c) + 1024),
                         lambda c: get(("k", 2 * h(c)), ("k", 2 * h(c) + 1)),
                         lambda c: [(1024 * h(c) + 128 * i, 8 * h(c) + i, 128) for i in range(8)],
                         lambda c: get(("v", 2 * h(c)), ("v", 2 * h(c) + 1)), post)

        def phase_ca(col0, vt0, post):
            return Phase(lambda c: (col0, col0 + TC), lambda c: get(*[("ck", i) for i in range(4)]),
                         lambda c: [(col0 + 128 * i, vt0 + i, min(128, TC - 128 * i)) for i in range(13)],
                         lambda c: get(*[("cv", i) for i in range(4)]), post)

        def units(ph, order):
            return [(ph, c, i % 2, hg) for i, c in enumerate(order) for hg in range(4)]

        def ctx_kv(c, col0, vt0, kr):
            n = min(512, TC - 512 * c)
            nt, w = (n + 127) // 128, min(n, 128)
            hold = {}

            def a():
                hold["l"] = q.go([(xn[0:w, 0:nt, :],
                                   I["ctx_1024"][0, 512 * c:512 * c + n, :].rearrange("(t p) d -> p t d", p=w))],
                                 get("xn_rd"))

            def b():
                z = transpose_in(xn, n, hold["l"])
                tok["xn_rd"] = [z]
            return [(0, a), (0, lambda: need_kv("ca")), (4, b),
                    (1, lambda: proj_k(col0 + 512 * c, n, ("ck", c), kr, 12)),
                    (1, lambda: proj_v(vt0 + 4 * c, n, ("cv", c), kr))]

        def mlp0(c):
            return ln_mod(c, 2) + mlp_chain(
                c, ACT.Gelu_apprx_tanh, 16, lambda c, s, z, lo=0, nt=4: residual_l0(c, s, z, 2, lo, nt))

        def mlp1(c):
            def store():
                q.go([(out[0, 512 * c:512 * c + 512, :].rearrange("(t p) d -> p t d", p=P),
                       x[:, 4 * c:4 * c + 4, :])], get(("x", c)))
            return [(4, lambda: x_to_xt(c))] + mlp_chain(
                c, ACT.Relu, 24, lambda c, s, z, lo=0, nt=4: residual_l1(c, s, z, (0, 0), lo, nt)) + ln_l1(c, 2) + [
                    (0, store)]

        ms = [big[:, 2048 * i:2048 * i + 2048].bitcast(I32) for i in range(2)]
        mb = big[:, 4096:4608].bitcast(BF16)
        macc = big[:, 5120:6144].bitcast(BF16)
        ones1 = sb("ones1", [P, 1], BF16)
        zc = big[0:1, 0:512]
        zt = big[0:1, 512:1024]
        br = sb("br", [1, 512], BF16)
        fl = sb("fl", [1, 8], F32)
        flag = sb("flag", [1, 1], I32)
        mask = I["mask_1x1xSxS_ik0"]
        t_one = pool.op(lambda e: e.memset(ones1[:], 1.0), consts)

        def scan(t, k):
            if k == 0:
                for u in ([0, 1] if t == 0 else [t + 1] if t + 1 < NT else []):
                    tok["ms", u % 2] = [q.go([(ms[u % 2], mask[0, 0, 128 * u:128 * u + 128, :])], get(("ms_rd", u % 2)))]
                    tok["ms_rd", u % 2] = []
            src = ms[t % 2][:, 512 * k:512 * k + 512]
            ac = macc[:, 512 * k:512 * k + 512]
            if k % 2:
                dst = ac if t == 0 else mb[:, 512 * (k // 2):512 * (k // 2) + 512]
                a = pool.op(lambda e: e.tensor_scalar(dst, src, 0.0, None, ALU.is_equal), get(("ms", t % 2)))
                if t:
                    a = pool.op(lambda e: e.tensor_tensor(ac, ac, dst, ALU.add), a, get(("macc", k)))
            elif t == 0:
                a = dve.op(lambda e: e.tensor_scalar(ac, src, 0.0, None, ALU.is_equal), get(("ms", t % 2)))
            else:
                a = dve.op(lambda e: e.scalar_tensor_tensor(ac, src, 0.0, ac, ALU.is_equal, ALU.add),
                            get(("ms", t % 2), ("macc", k)))
            add(("ms_rd", t % 2), a)
            tok["macc", k] = [a]

        def judge():
            sums = []
            for i in range(2):
                s, fr = M.take()
                for j in range(2):
                    z = pe.op(lambda e, i=i, j=j, s=s: e.matmul(
                        mslot(s)[0:1, j, :], ones1[:], macc[:, 1024 * i + 512 * j:1024 * i + 512 * j + 512],
                        start=True, stop=True), [get(("macc", k)) for k in range(4)], fr, t_one, sig=j == 1)
                if i == 0:
                    d = dve.op(lambda e, s=s: e.tensor_reduce(out=fl[:, 0:1], in_=mflat(s)[0:1, :], axis=AX.X,
                                                              op=ALU.add), z)
                else:
                    d1 = dve.op(lambda e, s=s: e.tensor_reduce(out=fl[:, 1:2], in_=mslot(s)[0:1, 0, :], axis=AX.X,
                                                               op=ALU.add), z)
                    d = dve.op(lambda e, s=s: e.tensor_copy(zc, mslot(s)[0:1, 1, :]), z)
                M.free[s] = d
            tok["w_rd"] = [z]
            n = float(T)
            b = dve.op(lambda e: e.tensor_scalar(br[:], zc, n - 0.5, NEG, ALU.is_gt, ALU.mult), d)
            c = dve.op(lambda e: e.tensor_scalar(zt, zc, -n, None, ALU.add), d)
            c = dve.op(lambda e: e.tensor_tensor(zt, zt, zc, ALU.mult), c)
            c = dve.op(lambda e: e.tensor_reduce(out=fl[:, 2:3], in_=zt, axis=AX.X, op=ALU.add), c)
            f = dve.op(lambda e: e.tensor_reduce(out=fl[:, 3:4], in_=zc, axis=AX.X, op=ALU.add), c)
            g = dve.op(lambda e: e.tensor_tensor(fl[:, 0:1], fl[:, 0:1], fl[:, 1:2], ALU.add), f, d1)
            g = dve.op(lambda e: e.tensor_scalar(fl[:, 4:5], fl[:, 0:1], 1536 * n - 0.5, None, ALU.is_gt), g)
            g = dve.op(lambda e: e.tensor_scalar(fl[:, 5:6], fl[:, 2:3], -0.5, None, ALU.is_gt), g)
            g = dve.op(lambda e: e.tensor_scalar(fl[:, 6:7], fl[:, 3:4], 512 * n - 0.5, None, ALU.is_lt), g)
            g = dve.op(lambda e: e.tensor_tensor(fl[:, 4:5], fl[:, 4:5], fl[:, 5:6], ALU.mult), g)
            g = dve.op(lambda e: e.tensor_tensor(flag[:], fl[:, 4:5], fl[:, 6:7], ALU.mult), g)
            tok["flag"] = [g]
            tok["br"] = [b]

        ln_stats(0, 1e-6)
        modulation(0)
        ln_xn(0)
        k3 = dve.op(lambda e: e.memset(Vt[:], 1.0))
        consts.extend(tok["s3_rd"] + [k3])
        ln_stats(1, 1e-6)
        mod_xt(0, 0)
        ln_xn(1)
        at.update(qf=PT[:, 6:8, :], quick=True)
        proj_k(0, 512, ("k", 0), None, 0)
        proj_q(0, 0, 0)
        at["xt"] = PT[:, 4:6, :]
        mod_xt(1, 0)
        proj_k(512, 512, ("k", 1), None, 0)
        load_wP(I["L0_xattn_attn_proj_w"])

        def first_v():
            at["xt"] = XT
            proj_v(0, 512, ("v", 0), None)

        def second_v():
            at.update(xt=PT[:, 4:6, :], qf=PT[:, 6:8, :], quick=True)
            proj_v(4, 512, ("v", 1), None)

        def second_q():
            proj_q(1, 1, 0)
            tok["pt_rd", 1] = get("xt_rd", "qf_rd")
            at.update(xt=XT, qf=Qf, quick=False)

        beside = [second_v, second_q, lambda: modulation(1), lambda: modulation(2),
                  lambda: gate_bias(0, I["L0_xattn_attn_proj_b"])]

        def post0(c, qs):
            if c == 0:
                return [out_l0(0, 0), q_l0(2, 0, 0)], []
            if c == 1:
                tok["half_rd", 0] = [(pe.sem, pe.n)]
                return [out_l0(1, 0), q_l0(3, 1, 0) + [(0, lambda: l0_weights("crs"))]], [
                    (99, kv_l0(0, 1)), (99, kv_l0(1, 1))]
            if c == 2:
                return [out_l0(2, 0), q_l0(2, 0, 1)], []
            return [], []

        def chains(f):
            def g(c, qs):
                u, l = f(c, qs)
                return [(0, x_) for x_ in u], l
            return g

        lazy.extend([(8, kv_l0(2, 0)), (8, kv_l0(3, 0))])
        side.extend([lambda t=t, k=k: scan(t, k) for t in range(NT) for k in range(4)])
        ph0 = phase_l0(0, chains(post0))
        ph1 = phase_l0(1, None)
        attention(units(ph0, (0, 1, 2, 3)), beyond=(ph1, 2, 0, 0), beside=beside,
                  early=[lambda: None, first_v])
        bg_until(999)
        for f in side:
            f()
        side.clear()
        tok["half_rd", 1] = [(pe.sem, pe.n)]
        judge()

        def fast():
            def crs_start():
                load_wP(I["L0_xattn_crs_proj_w"])
                gate_bias(1, I["L0_xattn_crs_proj_b"])
                load_mlp(I["L0_xattn_mlp_fc1_w"], I["L0_xattn_mlp_fc2_w"])
            urgent.extend([(0, out_l0(3, 0) + [(0, crs_start)]), (0, kv_l0(3, 1, 1)), (0, kv_l0(2, 1))])

            def sa_kv(kr):
                def weights():
                    need_kv("sa")
                    load_lnp(0, get("xn_rd"), (pool.sem, pool.n), (dve.sem, dve.n))

                def row():
                    bi = q.go([(KS[96:97, :, 0:512],
                                br[:].rearrange("a (p n) -> a p n", p=1).to_broadcast([1, H, 512]))], get("br"), kr)
                    tok["sak"] = get("sak0") + [bi]
                return [(0, weights), (4, lambda: x_to_xt(3)), (1, lambda: proj_k(0, 512, "sak0", kr, 8)), (0, row),
                        (1, lambda: proj_v(0, 512, "sav", kr))]

            def now():
                return [(pe.sem, pe.n)]

            def l1_out_start():
                plain_bias((1, 0), I["L1_xattn_sa_ob"])
                plain_bias((1, 1), I["L1_xattn_ca_ob"])
                load_lnp(1, (pool.sem, pool.n), (dve.sem, dve.n))

            def l1_mlp_start():
                plain_bias((0, 0), I["L1_xattn_b2"])
                load_lnp(2, (pool.sem, pool.n), (dve.sem, dve.n))
                load_mlp(I["L1_xattn_w1"], I["L1_xattn_w2"])

            def post(c, qs):
                if c == 2:
                    return [out_l0(2, 1) + [(0, lambda: gate_bias(2, I["L0_xattn_mlp_fc2_b"]))], q_l0(0, 0, 1)], [
                        (28, mlp0(2))]
                if c == 3:
                    return [out_l0(3, 1), q_l0(1, 1, 1)], [
                        (32, mlp0(3)), (32, sa_kv(now())), (44, ctx_kv(0, 512, 4, now())), (44, ctx_kv(3, 512, 4, now()))]
                if c == 0:
                    return [x_q(2, 0, "sa"), out_l0(0, 1)], [(36, mlp0(0))]
                return [x_q(3, 1, "sa"), out_l0(1, 1) + [(0, l1_out_start)]], [
                    (44, ctx_kv(1, 512, 4, now())), (44, ctx_kv(2, 512, 4, now())),
                    (48, mlp0(1) + [(0, l1_mlp_start)])]

            def post_sa(c, qs):
                o = out_l1(c, "sa")
                if c == 2:
                    return [x_q(0, 0, "sa"), o], []
                if c == 3:
                    return [x_q(2, 1, "ca"), o], []
                if c == 0:
                    return [o], [(48, x_q(1, 0, "sa"))]
                return [x_q(0, 0, "ca"), o], []

            def post_ca(c, qs):
                o = out_l1(c, "ca")
                return [x_q(3, 1, "ca"), o] if c == 2 else [x_q(1, 1, "ca"), o] if c == 3 else [o], [(99, mlp1(c))]

            p1, p3 = phase_l0(1, chains(post)), phase_ca(512, 4, chains(post_ca))
            p2 = Phase(lambda c: (0, 512), lambda c: tok["sak"], lambda c: [(128 * i, i, 128) for i in range(4)],
                       lambda c: tok["sav"], chains(post_sa))
            order = [(p1, 2), (p1, 3), (p1, 0), (p1, 1), (p2, 2), (p2, 3), (p2, 0), (p3, 2),
                     (p2, 1), (p3, 3), (p3, 0), (p3, 1)]
            attention([(ph, c, i % 2, hg) for i, (ph, c) in enumerate(order) for hg in range(4)], first=False)
            at["tail"] = True
            bg_until(999)
            at["tail"] = False

        def load_mask(c):
            w = [(pe.sem, pe.n)]
            ob_ = dve.op(lambda e: e.memset(onesB, 1.0), w)
            for t in range(4):
                for kc in range(4):
                    l = q.go([(mstg, mask[0, 0, 512 * c + 128 * t:512 * c + 128 * t + 128, 512 * kc:512 * kc + 512])],
                             get("mstg_rd"), w, ob_)
                    v = dve.op(lambda e: e.tensor_scalar(mbf, mstg, 0.0, None, ALU.is_equal), l, get("mbf_rd"))
                    tok["mstg_rd"] = [v]
                    s, fr = M.take()
                    o = mslot(s)[:, 0, 0:256].bitcast(BF16).rearrange("p (k n) -> p k n", k=4)
                    for k in range(4):
                        z = pe.op(lambda e, k=k, o=o: e.transpose(o[:, k, :], mbf[:, 128 * k:128 * k + 128], identB[:]),
                                  v, fr, ident)
                    tok["mbf_rd"] = [z]
                    d = dve.op(lambda e, kc=kc, t=t, o=o: e.tensor_copy(
                        maskT[:, 4 * kc:4 * kc + 4, 128 * t:128 * t + 128], o), z, w)
                    M.free[s] = d
            s, fr = M.take()
            for k in range(NT):
                z = pe.op(lambda e, k=k: e.matmul(mslot(s)[:, 0, :], onesB, maskT[:, k, :],
                                                  start=k == 0, stop=k == NT - 1), d, fr, ob_, sig=k == NT - 1)
            kp = dve.op(lambda e: e.tensor_scalar(keep, mslot(s)[:, 0, :], float(T) - 0.5, None, ALU.is_lt), z)
            M.free[s] = kp
            mm = dve.op(lambda e: e.tensor_tensor(
                maskT, maskT, keep.rearrange("p (o n) -> p o n", o=1).to_broadcast([P, NT, CH]), ALU.mult), kp)
            tok["maskT"] = [mm]
            t = dve.op(lambda e: e.tensor_tensor(
                QS[0:96, :, c % 2, :], QS[0:96, :, c % 2, :],
                keep[0:96, :].rearrange("p (o n) -> p o n", o=1).to_broadcast([96, H, CH]), ALU.mult),
                kp, get(("qs", c % 2)))
            tok["qs", c % 2] = [t]

        def general():
            none = lambda c, qs: ([], [])
            drain(out_l0(3, 0))
            load_wP(I["L0_xattn_crs_proj_w"])
            gate_bias(1, I["L0_xattn_crs_proj_b"])
            drain(kv_l0(2, 1) + kv_l0(3, 1, 1))

            def post(c, qs):
                return [(0, out_l0(c, 1))] + ([(0, q_l0(c - 2, qs, 1))] if c > 1 else []), []
            attention(units(phase_l0(1, post), (2, 3, 0, 1)), first=False)
            bg_until(999)
            tok["ks_rd"] = [(pe.sem, pe.n)]
            load_mlp(I["L0_xattn_mlp_fc1_w"], I["L0_xattn_mlp_fc2_w"])
            gate_bias(2, I["L0_xattn_mlp_fc2_b"])
            for c in range(4):
                drain(mlp0(c))
            for i in range(3):
                load_lnp(i, get("xn_rd"), (dve.sem, dve.n), (pool.sem, pool.n))
            need_kv("sa")
            plain_bias((1, 0), I["L1_xattn_sa_ob"])
            plain_bias((1, 1), I["L1_xattn_ca_ob"])
            plain_bias((0, 0), I["L1_xattn_b2"])
            kr = get("ks_rd")
            for c in range(4):
                x_to_xt(c)
                proj_k(512 * c, 512, ("k", c), kr, 8)
                proj_v(4 * c, 512, ("v", c), kr)
            p2 = Phase(lambda c: (0, T), lambda c: get(*[("k", i) for i in range(4)]),
                       lambda c: [(128 * i, i, 128) for i in range(16)], lambda c: get(*[("v", i) for i in range(4)]),
                       none, True)
            for c in range(4):
                drain(x_q(c, c % 2, "sa"))
                load_mask(c)
                attention([(p2, c, c % 2, hg) for hg in range(4)])
                drain(out_l1(c, "sa"))
            kr = [(pe.sem, pe.n)]
            load_mlp(I["L1_xattn_w1"], I["L1_xattn_w2"], kr, (dve.sem, dve.n))
            for c in range(4):
                drain(ctx_kv(c, 0, 0, kr))
            p3 = phase_ca(0, 0, none)
            for c in range(4):
                drain(x_q(c, c % 2, "ca"))
                attention([(p3, c, c % 2, hg) for hg in range(4)])
                drain(out_l1(c, "ca"))
                drain(mlp1(c))

        engs = (pe, act, dve, pool, sp)
        for e in engs:
            e.wait(get("flag"))
        state0 = ([(e.n, dict(e.seen)) for e in engs], (list(q.cnt), q.k), dict(tok), (M.i, list(M.free)),
                  (A.i, list(A.free)), (um[0], uo[0], nm4[0], nscr[0], unit0[0]))
        arms = []
        for arm in (fast, general):
            es, qst, tk, mst, ast, cn = state0
            main = [e.q for e in engs]
            for e, (n, seen) in zip(engs, es):
                e.n, e.seen, e.q = n, dict(seen), []
            q.cnt, q.k = list(qst[0]), qst[1]
            tok.clear()
            tok.update(tk)
            M.i, M.free, A.i, A.free = mst[0], list(mst[1]), ast[0], list(ast[1])
            um[0], uo[0], nm4[0], nscr[0], unit0[0] = cn
            arm()
            q.all_landed()
            arms.append([e.q for e in engs])
            for e, old in zip(engs, main):
                e.q = old
        for e, a, b in zip(engs, *arms):
            e.q.append(("b", flag[0:1, 0:1], a, b))

        block = ctx.enter_context(nc.Block())

        @block.sync
        def _(eng):
            sp.emit(eng)

        @block.gpsimd
        def _(eng):
            pool.emit(eng)

        @block.scalar
        def _(eng):
            act.emit(eng)

        @block.vector
        def _(eng):
            dve.emit(eng)

        @block.tensor
        def _(eng):
            pe.emit(eng)


_OUT = (1, 2048, 256)


def kernel(**inputs):
    import concourse.bacc as _bacc
    from concourse.bass_utils import run_bass_kernel_spmd as _run

    nc = _bacc.Bacc("TRN2", target_bir_lowering=False, num_devices=1, dynamic_dma_scratch_size=1024)
    arrays, aps = {}, {}
    for name, v in inputs.items():
        a = np.ascontiguousarray(v)
        arrays[f"in_{name}"] = a
        aps[name] = nc.dram_tensor(f"in_{name}", a.shape, mybir.dt.from_np(a.dtype), kind="ExternalInput").ap()
    o = nc.dram_tensor("out_0", _OUT, F32, kind="ExternalOutput").ap()
    xattn_kernel(nc, aps, o)
    r = _run(nc, [arrays], core_ids=[0])
    return r.results[0]["out_0"]
```
